# Optimizing a Trainium2 kernel written in Bass

```python
import numpy as np
import jax
import jax.numpy as jnp

def _softmax(x, axis=-1):
    return jax.nn.softmax(x, axis=axis)

def _gelu(x):
    return jax.nn.gelu(x, approximate=True)

def _silu(x):
    return jax.nn.silu(x)

def _sigmoid(x):
    return jax.nn.sigmoid(x)

def _layernorm(x, axis=-1, eps=1e-05):
    m = jnp.mean(x, axis=axis, keepdims=True)
    v = jnp.var(x, axis=axis, keepdims=True)
    return (x - m) / jnp.sqrt(v + eps)

def _scatter_add(tgt, idx, src, axis=0):
    return tgt.at[idx].add(src)

def _segment_sum(src, seg, n):
    return jax.ops.segment_sum(src, seg, n)
kernel_name = 'mk_flamingo_gated_d1_seqx_r4_2e12b6'

def setup_inputs(seed: int=0):
    np.random.seed(seed)
    _w = jnp.asarray

    def _rec_inputs():
        import jax
        import jax.numpy as jnp
        _rk = jax.random.key(seed)
        x = -0.0002928 + 1 * jax.random.normal(jax.random.fold_in(_rk, 1), (2, 512, 256), jnp.float32)
        _lenS = 512 - jax.random.randint(jax.random.fold_in(_rk, 7), (2,), 0, max(1, 512 // 4) + 1, jnp.int32)
        _lenS2 = 1024 - jax.random.randint(jax.random.fold_in(_rk, 8), (2,), 0, max(1, 1024 // 4) + 1, jnp.int32)
        _ctx_1024P = jax.random.normal(jax.random.fold_in(_rk, 11), (2, 16, 256), jnp.float32)
        _ctx_1024c = jax.random.dirichlet(jax.random.fold_in(_rk, 511), 0.3 * jnp.ones((16,), jnp.float32), (2, 1024))
        _ctx_1024t = jnp.einsum('bsk,bkd->bsd', _ctx_1024c, _ctx_1024P)
        _ctx_1024t = _ctx_1024t * jax.lax.rsqrt(jnp.mean(jnp.square(_ctx_1024t)) + 1e-12) * 0.953939
        ctx_1024 = -1.39393e-06 + 0.999914 * (_ctx_1024t + 0.3 * jax.random.normal(jax.random.fold_in(_rk, 611), (2, 1024, 256), jnp.float32))
        _validS = jnp.arange(512)[None, :] < _lenS[:, None]
        _validS2 = jnp.arange(1024)[None, :] < _lenS2[:, None]
        _causal = jnp.tril(jnp.ones((512, 512), dtype=bool))
        mask_BxSxS2_bk1 = jnp.broadcast_to(_validS2[:, None, :], (2, 512, 1024))
        _g = jax.random.normal(jax.random.fold_in(_rk, 9001), (2, 1), jnp.float32)
        _g = jnp.sign(_g) * jnp.maximum(jnp.abs(_g), 1.0) + (_g == 0) * 1.0
        g_xattn = _g[0]
        g_ffn = _g[1]
        return (x, ctx_1024, mask_BxSxS2_bk1, g_xattn, g_ffn)
    x, ctx_1024, mask_BxSxS2_bk1, g_xattn, g_ffn = _rec_inputs()

    def _L0_xattn_setup():
        import jax, jax.numpy as jnp
        import numpy as np
        DIM = 256
        HEADS = 16
        DIM_HEAD = 64
        INNER = HEADS * DIM_HEAD
        B, N = (2, 512)
        key = jax.random.key(seed)
        ks = jax.random.split(key, 8)
        q = jax.random.normal(ks[0], (B, N, DIM), dtype=jnp.float32)
        k = jax.random.normal(ks[1], (B, N, DIM), dtype=jnp.float32)
        v = jax.random.normal(ks[2], (B, N, DIM), dtype=jnp.float32)
        causal = jnp.triu(jnp.ones((N, N), dtype=jnp.bool_), k=1)
        mask = jnp.broadcast_to(causal, (B, N, N))
        s = 0.02
        Wq = jax.random.normal(ks[3], (DIM, INNER), dtype=jnp.float32) * s
        Wk = jax.random.normal(ks[4], (DIM, INNER), dtype=jnp.float32) * s
        Wv = jax.random.normal(ks[5], (DIM, INNER), dtype=jnp.float32) * s
        Wo = jax.random.normal(ks[6], (INNER, DIM), dtype=jnp.float32) * s
        bo = jnp.zeros((DIM,), dtype=jnp.float32)
        return {'q': q, 'k': k, 'v': v, 'mask': mask, 'Wq': Wq, 'Wk': Wk, 'Wv': Wv, 'Wo': Wo, 'bo': bo}
    _L0_xattn_all = _L0_xattn_setup()
    _L0_xattn_in = {k: v for k, v in _L0_xattn_all.items() if k in ('Wq', 'Wk', 'Wv', 'Wo', 'bo')}
    del _L0_xattn_all

    def _L0_ffn_setup():
        import jax, jax.numpy as jnp
        import numpy as np
        H = 256
        I = 256
        E = 8
        key = jax.random.key(seed)
        ks = jax.random.split(key, 8)
        s = 0.02
        x = jax.random.normal(ks[0], (4, 512, H), dtype=jnp.float32)
        Wg = jax.random.normal(ks[1], (H, E), dtype=jnp.float32) * s
        bg = jnp.zeros((E,), dtype=jnp.float32)
        W1 = jax.random.normal(ks[2], (E, H, I), dtype=jnp.float32) * s
        b1 = jnp.zeros((E, I), dtype=jnp.float32)
        W2 = jax.random.normal(ks[3], (E, I, H), dtype=jnp.float32) * s
        b2 = jnp.zeros((E, H), dtype=jnp.float32)
        return {'x': x, 'Wg': Wg, 'bg': bg, 'W1': W1, 'b1': b1, 'W2': W2, 'b2': b2}
    _L0_ffn_all = _L0_ffn_setup()
    _L0_ffn_in = {k: v for k, v in _L0_ffn_all.items() if k in ('Wg', 'bg', 'W1', 'b1', 'W2', 'b2')}
    del _L0_ffn_all
    return {'x': x, 'ctx_1024': ctx_1024, 'mask_BxSxS2_bk1': mask_BxSxS2_bk1, 'g_xattn': g_xattn, 'g_ffn': g_ffn, 'L0_xattn_Wq': _L0_xattn_in['Wq'], 'L0_xattn_Wk': _L0_xattn_in['Wk'], 'L0_xattn_Wv': _L0_xattn_in['Wv'], 'L0_xattn_Wo': _L0_xattn_in['Wo'], 'L0_xattn_bo': _L0_xattn_in['bo'], 'L0_ffn_Wg': _L0_ffn_in['Wg'], 'L0_ffn_bg': _L0_ffn_in['bg'], 'L0_ffn_W1': _L0_ffn_in['W1'], 'L0_ffn_b1': _L0_ffn_in['b1'], 'L0_ffn_W2': _L0_ffn_in['W2'], 'L0_ffn_b2': _L0_ffn_in['b2']}

def reference(x, ctx_1024, mask_BxSxS2_bk1, g_xattn, g_ffn, L0_xattn_Wq, L0_xattn_Wk, L0_xattn_Wv, L0_xattn_Wo, L0_xattn_bo, L0_ffn_Wg, L0_ffn_bg, L0_ffn_W1, L0_ffn_b1, L0_ffn_W2, L0_ffn_b2):
    import jax
    import jax.numpy as jnp

    def _L0_xattn_ref(q, k, v, mask, Wq, Wk, Wv, Wo, bo):
        import jax, jax.numpy as jnp
        import numpy as np
        DIM = 256
        HEADS = 16
        DIM_HEAD = 64
        INNER = HEADS * DIM_HEAD
        B, N = (2, 512)
        h, d = (HEADS, DIM_HEAD)
        scale = d ** (-0.5)
        b, n, _ = q.shape

        def heads_split(x):
            return x.reshape(b, -1, h, d).transpose(0, 2, 1, 3)
        qh = heads_split(q @ Wq)
        kh = heads_split(k @ Wk)
        vh = heads_split(v @ Wv)
        dots = jnp.einsum('bhid,bhjd->bhij', qh, kh) * scale
        mask_value = -jnp.finfo(dots.dtype).max
        dots = jnp.where(mask[:, None, :, :], mask_value, dots)
        attn = jax.nn.softmax(dots, axis=-1)
        out = jnp.einsum('bhij,bhjd->bhid', attn, vh)
        out = out.transpose(0, 2, 1, 3).reshape(b, n, h * d)
        out = out @ Wo + bo
        return out

    def _L0_ffn_ref(x, Wg, bg, W1, b1, W2, b2):
        import jax, jax.numpy as jnp
        import numpy as np
        H = 256
        I = 256
        E = 8
        B, S, Hd = x.shape
        xf = x.reshape(-1, Hd)
        logits = xf @ Wg + bg
        gates = jax.nn.softmax(logits, axis=-1)
        idx = jnp.argmax(gates, axis=-1)
        h = jax.nn.gelu(jnp.einsum('th,ehi->tei', xf, W1) + b1, approximate=False)
        y = jnp.einsum('tei,eih->teh', h, W2) + b2
        out = jnp.take_along_axis(y, idx[:, None, None], axis=1)[:, 0, :]
        return out.reshape(B, S, Hd)
    x = x + jnp.tanh(g_xattn[0]) * _L0_xattn_ref(_layernorm(x, axis=-1), ctx_1024, ctx_1024, mask_BxSxS2_bk1, L0_xattn_Wq, L0_xattn_Wk, L0_xattn_Wv, L0_xattn_Wo, L0_xattn_bo)
    x = x + jnp.tanh(g_ffn[0]) * _L0_ffn_ref(_layernorm(x, axis=-1), L0_ffn_Wg, L0_ffn_bg, L0_ffn_W1, L0_ffn_b1, L0_ffn_W2, L0_ffn_b2)
    return x

_drawn_inputs = setup_inputs


def setup_inputs(seed=0):
    import zlib

    import numpy as np

    out = dict(_drawn_inputs(seed))
    spreads = {'L0_xattn_bo': (0.0, 0.1),
     'L0_ffn_bg': (0.0, 0.1),
     'L0_ffn_b1': (0.0, 0.476),
     'L0_ffn_b2': (0.0, 0.1)}
    factors = {'L0_xattn_Wq': 7.689, 'L0_xattn_Wk': 7.007}
    for name, (base, spread) in spreads.items():
        noise = np.random.default_rng([zlib.crc32(name.encode()), seed]).standard_normal(out[name].shape)
        drawn = base * np.exp(spread * noise) if base else spread * noise
        out[name] = jnp.asarray(drawn.astype(out[name].dtype))
    for name, factor in factors.items():
        out[name] = (out[name] * factor).astype(out[name].dtype)
    return out
```

```python
from contextlib import ExitStack

import concourse.bass as bass
from concourse import mybir

ALU = mybir.AluOpType
ACT = mybir.ActivationFunctionType
AX = mybir.AxisListType
F32 = mybir.dt.float32
BF16 = mybir.dt.bfloat16
I32 = mybir.dt.int32
U8 = mybir.dt.uint8
P = 128
EPS = 1e-5


def flamingo_kernel(nc, x, ctx_in, mask, g_xattn, g_ffn, wq, wk, wv, wo, bo, wg, bg, w1, b1, w2, b2, out):
    B, N, D = x.shape
    S = ctx_in.shape[1]
    INNER = wq.shape[1]
    DH = 64
    H = INNER // DH
    E, _, I = w1.shape
    SCALE = DH ** -0.5
    BIG = 3.3e38
    DC = D // P
    IC = I // P
    QT = N // P
    TT = B * QT
    T = B * N
    CK = 256
    KT = CK // P
    NC = S // CK
    M = INNER // P
    PER = H
    UNITS = 1 + M // 2 + KT * INNER // 512
    UNITS_ACT, UNITS_DVE = (UNITS + 1) // 2, UNITS // 2

    with ExitStack() as stack:
        def sb(name, shape, dt=F32):
            return stack.enter_context(nc.sbuf_tensor(name, shape, dt))

        def sem(name):
            return stack.enter_context(nc.semaphore(name))

        wq_sb = sb("wq_sb", [P, DC, INNER])
        wk_sb = sb("wk_sb", [P, DC, INNER])
        wv_sb = sb("wv_sb", [P, DC, INNER])
        wo_sb = wq_sb[:].rearrange("p c n -> p (c n)").rearrange("p (m d) -> p m d", m=M)
        w1_sb = sb("w1_sb", [P, E, DC, I])
        w2_sb = sb("w2_sb", [P, E, IC, D])
        wg_sb = sb("wg_sb", [P, DC, E])
        b1_sb = sb("b1_sb", [P, E, IC])
        b2_sb = sb("b2_sb", [E, D])
        bg_sb = sb("bg_sb", [P, E])
        bo_sb = sb("bo_sb", [P, D])
        gate_in = sb("gate_in", [P, 2])
        gate = sb("gate", [P, 2])
        x_sb = sb("x_sb", [P, TT, D])
        mask_sb = sb("mask_sb", [P, TT, S], U8)
        ident = sb("ident", [P, P])
        ident_bf = sb("ident_bf", [P, P], BF16)
        ones = sb("ones", [P, 1])
        stats = sb("stats", [P, TT, 6])
        mv = sb("mv", [P, TT, 2])
        std = sb("std", [P, TT])
        rstd = sb("rstd", [P, TT])
        eps = sb("eps", [P, 1])
        xnT = sb("xnT", [P, DC, T])
        qT = sb("qT", [P, M, T])
        rowmin = sb("rowmin", [P, TT, NC])
        fullrow = sb("fullrow", [P, TT])
        chunkmin = sb("chunkmin", [P, B, NC])
        fullb = sb("fullb", [P, B])
        visit_p = sb("visit_p", [P, B, NC])
        visit = sb("visit", [1, B * NC], I32)
        ctx_sb = sb("ctx_sb", [P, KT, D])
        ctxT = sb("ctxT", [P, DC, CK])
        kT = sb("kT", [P, M, CK])
        v_sb = sb("v_sb", [P, KT, INNER])
        maskneg = sb("maskneg", [P, QT, CK], BF16)
        probs = sb("probs", [P, 2, QT, CK])
        pT = sb("pT", [P, 2, KT, N])
        xn = pT[:].rearrange("p a k n -> p (a k n)").rearrange("p (t d) -> p t d", d=D)
        negm_run = sb("negm_run", [P, QT, H])
        negm = sb("negm", [P, QT, H])
        cmax = sb("cmax", [P, 2, QT])
        dneg = sb("dneg", [P, QT, H])
        alpha = sb("alpha", [P, QT, H])
        lsum = sb("lsum", [P, QT, H])
        l_run = sb("l_run", [P, B, QT, H])
        o_part = sb("o_part", [P, QT, H, DH])
        o_run = sb("o_run", [P, B, QT, H, DH])
        rinv = sb("rinv", [P, B, QT, H])
        attnT = probs[:].rearrange("p a q k -> p (a q k)").rearrange("p (a m k) -> p a m k", a=2, m=M)
        logits = sb("logits", [P, TT, E])
        lmax = sb("lmax", [P, TT])
        first_w = sb("first_w", [P, E])
        ismax = sb("ismax", [P, TT, E])
        onehot = sb("onehot", [P, TT, E])
        onehot_g = sb("onehot_g", [P, TT, E])
        onehotT = kT[:].rearrange("p m k -> p (m k)")[0:E, 0:T]
        hT = pT

        bank = [stack.enter_context(nc.psum_tensor(f"bank{i}", [P, 512], F32)) for i in range(8)]

        s_x = [sem(f"s_x{b}") for b in range(B)]
        s_wq = sem("s_wq")
        s_mask = sem("s_mask")
        s_wkv = sem("s_wkv")
        s_small = sem("s_small")
        s_wlate = sem("s_wlate")
        s_ctx = sem("s_ctx")
        ident_ready = sem("ident_ready")
        pool_step = sem("pool_step")
        var_ready = sem("var_ready")
        std_ready = sem("std_ready")
        ln_ready = sem("ln_ready")
        dve_step = sem("dve_step")
        pro_ps = sem("pro_ps")
        pro_act = sem("pro_act")
        pro_dve = sem("pro_dve")
        visit_part = sem("visit_part")
        visit_ps = sem("visit_ps")
        visit_ready = sem("visit_ready")
        gate_ready = sem("gate_ready")
        xb_ready = sem("xb_ready")
        proj_ps = sem("proj_ps")
        proj_act = sem("proj_act")
        proj_dve = sem("proj_dve")
        mask_ready = sem("mask_ready")
        scores_ready = sem("scores_ready")
        cmax_done = sem("cmax_done")
        negm_ready = sem("negm_ready")
        l_scaled = sem("l_scaled")
        l_summed = sem("l_summed")
        probs_ready = sem("probs_ready")
        ptrans_ready = sem("ptrans_ready")
        pT_act = sem("pT_act")
        pT_dve = sem("pT_dve")
        o_ready = sem("o_ready")
        o_taken = sem("o_taken")
        dneg_ready = sem("dneg_ready")
        alpha_ready = sem("alpha_ready")
        o_summed = sem("o_summed")
        state_init = sem("state_init")
        rinv_ready = sem("rinv_ready")
        o_normed = sem("o_normed")
        at_ps = sem("at_ps")
        at_act = sem("at_act")
        at_dve = sem("at_dve")
        wo_ready = sem("wo_ready")
        x2_ready = sem("x2_ready")
        xn2_ready = sem("xn2_ready")
        xt2_ps = sem("xt2_ps")
        xt2_sb = sem("xt2_sb")
        logit_ps = sem("logit_ps")
        onehot_ready = sem("onehot_ready")
        oht_ps = sem("oht_ps")
        oht_sb = sem("oht_sb")
        b2_ps = sem("b2_ps")
        b2_added = sem("b2_added")
        h_ps = sem("h_ps")
        h_ready = sem("h_ready")
        y_ps = sem("y_ps")
        y_added = sem("y_added")
        s_out = sem("s_out")

        def pro_dst(u):
            if u < 4:
                return xnT[:, u // 2, (u % 2) * 512:(u % 2 + 1) * 512]
            u -= 4
            return qT[:, u // B, (u % B) * 512:(u % B + 1) * 512]

        def proj_dst(u):
            if u == 0:
                return ctxT[:].rearrange("p c k -> p (c k)")
            u -= 1
            if u < M // 2:
                return kT[:, 2 * u:2 * u + 2, :].rearrange("p m k -> p (m k)")
            u -= M // 2
            half = INNER // 512
            return v_sb[:, u // half, (u % half) * 512:(u % half + 1) * 512]

        def take_wo(tt, then, norm):
            nc.vector.wait_ge(wo_ready, tt + 1)
            if tt == 0:
                nc.vector.wait_ge(xb_ready, 1)
            then(nc.vector.scalar_tensor_tensor(x_sb[:, tt, :], bank[6 + tt % 2][:, 0:D], gate[:, 0:1], x_sb[:, tt, :],
                                                ALU.mult, ALU.add))
            norm(x_sb, [tt], xn2_ready)

        block = stack.enter_context(nc.Block())

        @block.sync
        def _(sp):
            for b in range(B):
                sp.dma_start(x_sb[:, b * QT:(b + 1) * QT, :],
                             x[b].rearrange("(q p) d -> p q d", p=P)).then_inc(s_x[b], 16)
            sp.dma_start(wq_sb[:], wq.rearrange("(c p) n -> p c n", p=P)).then_inc(s_wq, 16)
            sp.dma_start(mask_sb[:], mask.rearrange("b (q p) k -> p (b q) k", p=P)).then_inc(s_mask, 16)
            sp.dma_start(wk_sb[:], wk.rearrange("(c p) n -> p c n", p=P)).then_inc(s_wkv, 16)
            sp.dma_start(wv_sb[:], wv.rearrange("(c p) n -> p c n", p=P)).then_inc(s_wkv, 16)
            sp.wait_ge(visit_ready, 1)
            done = sp.alloc_register("sp_done")
            sp.reg_mov(done, 0)
            for b in range(B):
                with sp.Fori(0, NC) as c:
                    flag = sp.value_load(visit[0:1, bass.ds(c + b * NC, 1)], min_val=0, max_val=1)
                    with sp.If(flag > 0):
                        n = sp.snap(done)
                        sp.wait_ge(proj_ps, n * UNITS + 1)
                        sp.dma_start(ctx_sb[:], ctx_in[b, bass.ds(c * CK, CK), :]
                                     .rearrange("(t p) d -> p t d", p=P)).then_inc(s_ctx, 16)
                        sp.reg_add(done, done, 1)
                    with sp.Else():
                        sp.nop()
            sp.wait_ge(pro_ps, 4 + M * B)
            sp.dma_start(wo_sb, wo.rearrange("(m p) d -> p m d", p=P)).then_inc(s_wlate, 16)
            sp.dma_start(w1_sb[:], w1.rearrange("e (c p) i -> p e c i", p=P)).then_inc(s_wlate, 16)
            sp.dma_start(w2_sb[:], w2.rearrange("e (c p) d -> p e c d", p=P)).then_inc(s_wlate, 16)
            for tt in range(TT):
                sp.wait_ge(y_added, (E - 1) * TT + tt + 1)
                b, q = tt // QT, tt % QT
                sp.dma_start(out[b, q * P:(q + 1) * P, :], x_sb[:, tt, :]).then_inc(s_out, 16)
            sp.wait_ge(s_out, 16 * TT)

        @block.gpsimd
        def _(pool):
            pool.sem_inc(o_summed, 1)
            nc.gpsimd.memset(ident[:], 0.0).then_inc(pool_step, 1)
            nc.gpsimd.memset(ident_bf[:], 0.0).then_inc(pool_step, 1)
            nc.gpsimd.memset(eps[:], EPS).then_inc(ident_ready, 1)
            nc.gpsimd.memset(ones[:], 1.0).then_inc(ident_ready, 1)
            for e in range(E):
                nc.gpsimd.memset(first_w[:, e:e + 1], float(E - e)).then_inc(ident_ready, 1)
            pool.wait_ge(pool_step, 2)
            for m in (ident, ident_bf):
                nc.gpsimd.affine_select(out=m[:], in_=m[:], compare_op=ALU.not_equal, fill=1.0, base=0,
                                        pattern=[[-1, P]], channel_multiplier=1).then_inc(ident_ready, 1)
            nc.gpsimd.memset(o_run[:], 0.0).then_inc(state_init, 1)
            pool.wait_ge(gate_ready, 1)
            pool.wait_ge(ln_ready, TT)
            nc.gpsimd.tensor_scalar(bo_sb[:], bo_sb[:], gate[:, 0:1], None, ALU.mult).then_inc(pool_step, 1)
            pool.wait_ge(pool_step, 3)
            nc.gpsimd.tensor_tensor(x_sb[:], x_sb[:], bo_sb[:].unsqueeze(1).broadcast_to([P, TT, D]),
                                    ALU.add).then_inc(xb_ready, 1)
            pool.wait_ge(state_init, 1)
            pool.wait_ge(visit_ready, 1)
            done = pool.alloc_register("pool_done")
            pool.reg_mov(done, 0)
            for b in range(B):
                with pool.Fori(0, NC) as c:
                    flag = pool.value_load(visit[0:1, bass.ds(c + b * NC, 1)], min_val=0, max_val=1)
                    with pool.If(flag > 0):
                        n = pool.snap(done)
                        pool.wait_ge(alpha_ready, n + 1)
                        o = o_run[:, b].rearrange("p q h d -> p (q h) d")
                        a = alpha[:].rearrange("p q h -> p (q h)").unsqueeze(2).broadcast_to([P, QT * H, DH])
                        nc.gpsimd.tensor_tensor(o, o, a, ALU.mult).then_inc(o_summed, 1)
                        pool.wait_ge(o_summed, n * 2 + 2)
                        pool.wait_ge(o_taken, (n + 1) * PER + 1)
                        nc.gpsimd.tensor_tensor(o, o, o_part[:].rearrange("p q h d -> p (q h) d"),
                                                ALU.add).then_inc(o_summed, 1)
                        pool.wait_ge(o_summed, n * 2 + 3)
                        pool.reg_add(done, done, 1)
                    with pool.Else():
                        pool.nop()
                pool.wait_ge(rinv_ready, b + 1)
                o = o_run[:, b].rearrange("p q h d -> p (q h) d")
                r = rinv[:, b].rearrange("p q h -> p (q h)").unsqueeze(2).broadcast_to([P, QT * H, DH])
                nc.gpsimd.tensor_tensor(o, o, r, ALU.mult).then_inc(o_normed, 1)

        @block.scalar
        def _(act):
            act.dma_start(gate_in[:, 0:1], g_xattn.unsqueeze(0).broadcast_to([P, 1])).then_inc(s_small, 16)
            act.dma_start(gate_in[:, 1:2], g_ffn.unsqueeze(0).broadcast_to([P, 1])).then_inc(s_small, 16)
            act.dma_start(bo_sb[:], bo.unsqueeze(0).broadcast_to([P, D])).then_inc(s_small, 16)
            act.dma_start(bg_sb[:], bg.unsqueeze(0).broadcast_to([P, E])).then_inc(s_small, 16)
            act.dma_start(b1_sb[:], b1.rearrange("e (c p) -> p e c", p=P),
                          allow_slow_non_contiguous=True).then_inc(s_small, 16)
            act.dma_start(b2_sb[:], b2).then_inc(s_small, 16)
            act.dma_start(wg_sb[:], wg.rearrange("(c p) e -> p c e", p=P)).then_inc(s_small, 16)
            act.wait_ge(ident_ready, E + 4)
            for b in range(B):
                act.wait_ge(var_ready, b + 1)
                nc.scalar.activation(std[:, b * QT:(b + 1) * QT], mv[:, b * QT:(b + 1) * QT, 1], ACT.Sqrt,
                                     bias=eps[:]).then_inc(std_ready, 1)
            act.wait_ge(s_small, 16 * 7)
            nc.scalar.activation(gate[:], gate_in[:], ACT.Tanh).then_inc(gate_ready, 1)
            for u in range(0, 4 + M * B, 2):
                act.wait_ge(pro_ps, u + 1)
                nc.scalar.copy(pro_dst(u), bank[u % 4][:]).then_inc(pro_act, 1)
            act.wait_ge(visit_ready, 1)
            done = act.alloc_register("act_done")
            act.reg_mov(done, 0)
            for b in range(B):
                with act.Fori(0, NC) as c:
                    flag = act.value_load(visit[0:1, bass.ds(c + b * NC, 1)], min_val=0, max_val=1)
                    with act.If(flag > 0):
                        n = act.snap(done)
                        units = n * UNITS
                        g = n * PER
                        for u in range(0, UNITS, 2):
                            act.wait_ge(proj_ps, units + (u + 2))
                            nc.scalar.copy(proj_dst(u), bank[u % 4][:]).then_inc(proj_act, 1)

                        def take_pT(h):
                            act.wait_ge(ptrans_ready, g * 2 + (2 * h + 1))
                            act.wait_ge(o_ready, g + (max(h - 1, 0) + 1))
                            nc.scalar.copy(pT[:, h % 2, 0, :], bank[4][:]).then_inc(pT_act, 1)

                        for h in range(H):
                            act.wait_ge(negm_ready, g + (h + 1))
                            for q in range(QT):
                                if q == QT // 2 and h >= 1:
                                    take_pT(h - 1)
                                if q == 0 and h >= 2:
                                    act.wait_ge(ptrans_ready, g * 2 + 2 * (h - 1))
                                s = bank[2 * (h % 2) + q // 2][:, (q % 2) * CK:(q % 2 + 1) * CK]
                                last = nc.scalar.activation(probs[:, h % 2, q, :], s, ACT.Exp,
                                                            bias=negm[:, q, h:h + 1], scale=SCALE,
                                                            accum_out=lsum[:, q, h:h + 1])
                            last.then_inc(probs_ready, 1)
                        take_pT(H - 1)
                        act.wait_ge(dneg_ready, n + 1)
                        act.wait_ge(o_summed, n * 2 + 1)
                        nc.scalar.activation(alpha[:], dneg[:], ACT.Exp).then_inc(alpha_ready, 1)
                        act.reg_add(done, done, 1)
                    with act.Else():
                        act.nop()

            def take_std(tt):
                act.wait_ge(var_ready, B + tt + 1)
                nc.scalar.activation(std[:, tt:tt + 1], mv[:, tt, 1:2], ACT.Sqrt, bias=eps[:]).then_inc(std_ready, 1)

            for tt in range(TT):
                act.wait_ge(at_ps, 2 * tt + 1)
                if tt >= 2:
                    act.wait_ge(wo_ready, tt - 1)
                nc.scalar.copy(attnT[:, tt % 2, 0:M // 2, :],
                               bank[2 * (tt % 2)][:].rearrange("p (m k) -> p m k", k=P)).then_inc(at_act, 1)
                if tt >= 1:
                    take_std(tt - 1)
            take_std(TT - 1)
            for u in range(0, 2 * DC, 1):
                act.wait_ge(xt2_ps, u + 1)
                nc.scalar.copy(xnT[:, u // 2, (u % 2) * 512:(u % 2 + 1) * 512], bank[u % 4][:]).then_inc(xt2_sb, 1)
            k = 0
            for e in range(E):
                for tb in range(T // 512):
                    for ic in range(IC):
                        act.wait_ge(h_ps, k + 1)
                        if k >= 2 * IC:
                            act.wait_ge(y_ps, ((k // IC) - 1) * 4)
                        nc.scalar.activation(hT[:, (k // IC) % 2, ic, :], bank[k % 4][:], ACT.Gelu,
                                             bias=b1_sb[:, e, ic:ic + 1]).then_inc(h_ready, 1)
                        k += 1

        @block.vector
        def _(dve):
            steps, stds = [0], [0]
            dve.sem_inc(o_taken, 1)

            def then(ins):
                steps[0] += 1
                ins.then_inc(dve_step, 1)
                dve.wait_ge(dve_step, steps[0])

            def norm(src, tiles, ready):
                for t in tiles:
                    last = nc.vector.bn_stats(stats[:, t, :], src[:, t, :])
                then(last)
                for t in tiles:
                    last = nc.vector.bn_aggr(mv[:, t, :], stats[:, t, :])
                last.then_inc(var_ready, 1)
                a, z = tiles[0], tiles[-1] + 1
                stds[0] += 1
                dve.wait_ge(std_ready, stds[0])
                then(nc.vector.reciprocal(rstd[:, a:z], std[:, a:z]))
                for t in tiles:
                    nc.vector.tensor_scalar(xn[:, t, :], src[:, t, :], mv[:, t, 0:1], rstd[:, t:t + 1],
                                            ALU.subtract, ALU.mult).then_inc(ready, 1)

            for b in range(B):
                dve.wait_ge(s_x[b], 16)
                norm(x_sb, list(range(b * QT, (b + 1) * QT)), ln_ready)
            for u in range(1, 4, 2):
                dve.wait_ge(pro_ps, u + 1)
                nc.vector.tensor_copy(pro_dst(u), bank[u % 4][:]).then_inc(pro_dve, 1)
            dve.wait_ge(s_mask, 16)
            for t in range(TT):
                then(nc.vector.tensor_reduce(rowmin[:, t, :], mask_sb[:, t, :].rearrange("p (c k) -> p c k", k=CK),
                                             AX.X, ALU.min))
                u = 5 + 2 * t
                dve.wait_ge(pro_ps, u + 1)
                nc.vector.tensor_copy(pro_dst(u), bank[u % 4][:]).then_inc(pro_dve, 1)
            nc.vector.tensor_reduce(chunkmin[:], rowmin[:].rearrange("p (b q) c -> p b c q", b=B), AX.X, ALU.min)
            then(nc.vector.tensor_reduce(fullrow[:], rowmin[:], AX.X, ALU.min))
            then(nc.vector.tensor_reduce(fullb[:], fullrow[:].rearrange("p (b q) -> p b q", b=B), AX.X, ALU.max))
            nc.vector.tensor_tensor(visit_p[:], fullb[:].unsqueeze(2).broadcast_to([P, B, NC]), chunkmin[:],
                                    ALU.subtract).then_inc(visit_part, 1)
            dve.wait_ge(visit_ps, 1)
            nc.vector.tensor_scalar(visit[:], bank[4][0:1, 0:B * NC], -P + 0.5, None, ALU.is_gt)\
                .then_inc(visit_ready, 1)
            dve.wait_ge(visit_ready, 1)
            done = dve.alloc_register("dve_done")
            dve.reg_mov(done, 0)
            for b in range(B):
                nc.vector.memset(l_run[:, b], 0.0)
                nc.vector.memset(negm_run[:], BIG * SCALE)
                with dve.Fori(0, NC) as c:
                    flag = dve.value_load(visit[0:1, bass.ds(c + b * NC, 1)], min_val=0, max_val=1)
                    with dve.If(flag > 0):
                        n = dve.snap(done)
                        units = n * UNITS
                        g = n * PER
                        dve.wait_ge(scores_ready, g + 1)
                        nc.vector.tensor_scalar(maskneg[:], mask_sb[:, b * QT:(b + 1) * QT, bass.ds(c * CK, CK)],
                                                -BIG, None, ALU.mult).then_inc(mask_ready, 1)
                        for u in range(1, UNITS, 2):
                            dve.wait_ge(proj_ps, units + (u + 2))
                            nc.vector.tensor_copy(proj_dst(u), bank[u % 4][:]).then_inc(proj_dve, 1)

                        def take_max(h):
                            dve.wait_ge(scores_ready, g + (h + 2))
                            for i in range(2):
                                last = nc.vector.tensor_reduce(
                                    cmax[:, h % 2, 2 * i:2 * i + 2],
                                    bank[2 * (h % 2) + i][:].rearrange("p (q k) -> p q k", k=CK), AX.X, ALU.max)
                            last.then_inc(cmax_done, 1)
                            dve.wait_ge(cmax_done, g + (h + 1))
                            nc.vector.scalar_tensor_tensor(negm[:, :, h], cmax[:, h % 2, :], -SCALE,
                                                           negm_run[:, :, h], ALU.mult, ALU.min)\
                                .then_inc(negm_ready, 1)

                        def take_pT(h):
                            dve.wait_ge(ptrans_ready, g * 2 + (2 * h + 2))
                            dve.wait_ge(o_ready, g + (max(h - 1, 0) + 1))
                            nc.vector.tensor_copy(pT[:, h % 2, 1, :], bank[5][:]).then_inc(pT_dve, 1)

                        def take_o(h):
                            dve.wait_ge(o_ready, g + (h + 2))
                            if h == 0:
                                dve.wait_ge(o_summed, n * 2 + 1)
                            nc.vector.tensor_copy(o_part[:, :, h, :],
                                                  bank[6 + h % 2][:, 0:QT * DH].rearrange("p (q d) -> p q d", d=DH))\
                                .then_inc(o_taken, 1)

                        take_max(0)
                        for h in range(H):
                            if h + 1 < H:
                                take_max(h + 1)
                            take_pT(h)
                            if h >= 1:
                                take_o(h - 1)
                        nc.vector.tensor_tensor(dneg[:], negm[:], negm_run[:], ALU.subtract).then_inc(dneg_ready, 1)
                        take_o(H - 1)
                        dve.wait_ge(alpha_ready, n + 1)
                        nc.vector.tensor_copy(negm_run[:], negm[:])
                        nc.vector.tensor_tensor(l_run[:, b], l_run[:, b], alpha[:], ALU.mult).then_inc(l_scaled, 1)
                        dve.wait_ge(l_scaled, n + 1)
                        nc.vector.tensor_tensor(l_run[:, b], l_run[:, b], lsum[:], ALU.add).then_inc(l_summed, 1)
                        dve.wait_ge(l_summed, n + 1)
                        dve.reg_add(done, done, 1)
                    with dve.Else():
                        dve.nop()
                nc.vector.reciprocal(rinv[:, b], l_run[:, b]).then_inc(rinv_ready, 1)
            for tt in range(TT):
                dve.wait_ge(at_ps, 2 * tt + 2)
                if tt >= 2:
                    dve.wait_ge(wo_ready, tt - 1)
                nc.vector.tensor_copy(attnT[:, tt % 2, M // 2:M, :], bank[2 * (tt % 2) + 1][:].rearrange("p (m k) -> p m k", k=P)).then_inc(at_dve, 1)
                if tt >= 1:
                    take_wo(tt - 1, then, norm)
            take_wo(TT - 1, then, norm)
            dve.wait_ge(logit_ps, 1)
            then(nc.vector.tensor_tensor(logits[:], bank[6][:, 0:TT * E].rearrange("p (t e) -> p t e", e=E),
                                         bg_sb[:].unsqueeze(1).broadcast_to([P, TT, E]), ALU.add))
            then(nc.vector.tensor_reduce(lmax[:], logits[:], AX.X, ALU.max))
            then(nc.vector.tensor_tensor(ismax[:], logits[:], lmax[:].unsqueeze(2).broadcast_to([P, TT, E]),
                                         ALU.is_equal))
            then(nc.vector.tensor_tensor(ismax[:], ismax[:], first_w[:].unsqueeze(1).broadcast_to([P, TT, E]),
                                         ALU.mult))
            then(nc.vector.tensor_reduce(lmax[:], ismax[:], AX.X, ALU.max))
            nc.vector.tensor_tensor(onehot[:], ismax[:], lmax[:].unsqueeze(2).broadcast_to([P, TT, E]),
                                    ALU.is_equal).then_inc(onehot_ready, 1)
            dve.wait_ge(onehot_ready, 1)
            then(nc.vector.tensor_scalar(onehot_g[:], onehot[:], gate[:, 1:2], None, ALU.mult))
            for i in range(2):
                dve.wait_ge(oht_ps, i + 1)
                nc.vector.tensor_copy(onehotT[:, i * 512:(i + 1) * 512], bank[4 + i][0:E, :]).then_inc(oht_sb, 1)
            for tt in range(TT):
                dve.wait_ge(b2_ps, tt + 1)
                nc.vector.scalar_tensor_tensor(x_sb[:, tt, :], bank[6 + tt % 2][:, 0:D], gate[:, 1:2], x_sb[:, tt, :],
                                               ALU.mult, ALU.add).then_inc(b2_added, 1)
            k = 0
            for e in range(E):
                for tt in range(TT):
                    dve.wait_ge(y_ps, k + 1)
                    if e == 0:
                        dve.wait_ge(b2_added, TT)
                    else:
                        dve.wait_ge(y_added, k - TT + 1)
                    nc.vector.scalar_tensor_tensor(x_sb[:, tt, :], bank[4 + k % 4][:, 0:D], onehot_g[:, tt, e:e + 1],
                                                   x_sb[:, tt, :], ALU.mult, ALU.add).then_inc(y_added, 1)
                    k += 1

        @block.tensor
        def _(pe):
            pe.sem_inc(proj_ps, 1)
            pe.sem_inc(scores_ready, 1)
            pe.sem_inc(o_ready, 1)
            pe.wait_ge(ident_ready, E + 4)
            for u in range(4):
                c, half = u // 2, u % 2
                pe.wait_ge(ln_ready, 4 * (half + 1))
                for i in range(4):
                    last = nc.tensor.transpose(bank[u][:, i * P:(i + 1) * P],
                                               xn[:, half * 4 + i, c * P:(c + 1) * P], ident[:])
                last.then_inc(pro_ps, 1)
            pe.wait_ge(pro_act, 2)
            pe.wait_ge(pro_dve, 2)
            pe.wait_ge(s_wq, 16)
            for u in range(4, 4 + M * B):
                m, half = (u - 4) // B, (u - 4) % B
                if u >= 8:
                    pe.wait_ge(pro_dve if u % 2 else pro_act, (u - 4) // 2 + 1)
                for c in range(DC):
                    last = nc.tensor.matmul(bank[u % 4][:], wq_sb[:, c, m * P:(m + 1) * P],
                                            xnT[:, c, half * 512:(half + 1) * 512], start=(c == 0), stop=(c == DC - 1))
                last.then_inc(pro_ps, 1)
            pe.wait_ge(visit_part, 1)
            nc.tensor.matmul(bank[4][0:1, 0:B * NC], ones[:], visit_p[:].rearrange("p b c -> p (b c)"),
                             start=True, stop=True).then_inc(visit_ps, 1)
            pe.wait_ge(visit_ready, 1)
            pe.wait_ge(pro_act, (4 + M * B) // 2)
            pe.wait_ge(pro_dve, (4 + M * B) // 2)
            pe.wait_ge(s_wkv, 32)
            done = pe.alloc_register("pe_done")
            pe.reg_mov(done, 0)
            for b in range(B):
                with pe.Fori(0, NC) as cc:
                    flag = pe.value_load(visit[0:1, bass.ds(cc + b * NC, 1)], min_val=0, max_val=1)
                    with pe.If(flag > 0):
                        n = pe.snap(done)
                        g = n * PER
                        ua, ud = n * UNITS_ACT, n * UNITS_DVE
                        pe.wait_ge(s_ctx, n * 16 + 16)
                        for c in range(DC):
                            for t in range(KT):
                                last = nc.tensor.transpose(bank[0][:, c * CK + t * P:c * CK + (t + 1) * P],
                                                           ctx_sb[:, t, c * P:(c + 1) * P], ident[:])
                        last.then_inc(proj_ps, 1)
                        pe.wait_ge(proj_act, ua + 1)
                        for u in range(1, UNITS):
                            if u >= 4:
                                pe.wait_ge(proj_dve if u % 2 else proj_act,
                                           (ud if u % 2 else ua) + ((u - 4) // 2 + 1))
                            if u <= M // 2:
                                for i in range(2):
                                    m = 2 * (u - 1) + i
                                    for c in range(DC):
                                        last = nc.tensor.matmul(bank[u % 4][:, i * CK:(i + 1) * CK],
                                                                wk_sb[:, c, m * P:(m + 1) * P], ctxT[:, c, :],
                                                                start=(c == 0), stop=(c == DC - 1))
                            else:
                                v = u - 1 - M // 2
                                t, half = v // (INNER // 512), v % (INNER // 512)
                                for c in range(DC):
                                    last = nc.tensor.matmul(bank[u % 4][:], ctxT[:, c, t * P:(t + 1) * P],
                                                            wv_sb[:, c, half * 512:(half + 1) * 512],
                                                            start=(c == 0), stop=(c == DC - 1))
                            last.then_inc(proj_ps, 1)
                        pe.wait_ge(proj_act, ua + UNITS_ACT)
                        pe.wait_ge(proj_dve, ud + UNITS_DVE)
                        pe.wait_ge(mask_ready, n + 1)

                        def scores(h):
                            if h >= 2:
                                pe.wait_ge(probs_ready, g + (h - 1))
                            r = (h % 2) * DH
                            for q in range(QT):
                                s = bank[2 * (h % 2) + q // 2][:, (q % 2) * CK:(q % 2 + 1) * CK]
                                nc.tensor.matmul(s, qT[r:r + DH, h // 2, b * N + q * P:b * N + (q + 1) * P],
                                                 kT[r:r + DH, h // 2, :], start=True, stop=False)
                                last = nc.tensor.matmul(s, ident_bf[:], maskneg[:, q, :], start=False, stop=True)
                            last.then_inc(scores_ready, 1)

                        def transposes(h):
                            pe.wait_ge(probs_ready, g + (h + 1))
                            if h >= 1:
                                pe.wait_ge(pT_act, g + h)
                                pe.wait_ge(pT_dve, g + h)
                            for t in range(KT):
                                for q in range(QT):
                                    last = nc.tensor.transpose(bank[4 + t][:, q * P:(q + 1) * P],
                                                               probs[:, h % 2, q, t * P:(t + 1) * P], ident[:])
                                last.then_inc(ptrans_ready, 1)

                        def values(h):
                            pe.wait_ge(pT_act, g + (h + 1))
                            pe.wait_ge(pT_dve, g + (h + 1))
                            pe.wait_ge(o_taken, g + (max(h - 1, 0) + 1))
                            for q in range(QT):
                                for t in range(KT):
                                    last = nc.tensor.matmul(bank[6 + h % 2][:, q * DH:(q + 1) * DH],
                                                            pT[:, h % 2, t, q * P:(q + 1) * P],
                                                            v_sb[:, t, h * DH:(h + 1) * DH],
                                                            start=(t == 0), stop=(t == KT - 1))
                            last.then_inc(o_ready, 1)

                        scores(0)
                        for h in range(H):
                            if h + 1 < H:
                                scores(h + 1)
                            if h >= 1:
                                values(h - 1)
                            transposes(h)
                        values(H - 1)
                        pe.reg_add(done, done, 1)
                    with pe.Else():
                        pe.nop()
            pe.wait_ge(s_wlate, 48)
            n = pe.snap(done)
            pe.wait_ge(o_taken, n * PER + 1)

            def attn_T(tt):
                b, q = tt // QT, tt % QT
                pe.wait_ge(o_normed, b + 1)
                if tt >= 2:
                    pe.wait_ge(at_act, tt - 1)
                    pe.wait_ge(at_dve, tt - 1)
                for m in range(M):
                    last = nc.tensor.transpose(bank[2 * (tt % 2) + m // 4][:, (m % 4) * P:(m % 4 + 1) * P],
                                               o_run[:, b, q, 2 * m:2 * m + 2, :].rearrange("p h d -> p (h d)"),
                                               ident[:])
                    if m % 4 == 3:
                        last.then_inc(at_ps, 1)

            def project(tt):
                pe.wait_ge(at_act, tt + 1)
                pe.wait_ge(at_dve, tt + 1)
                if tt >= 2:
                    pe.wait_ge(xn2_ready, tt - 1)
                for m in range(M):
                    last = nc.tensor.matmul(bank[6 + tt % 2][:, 0:D], attnT[:, tt % 2, m, :], wo_sb[:, m, :],
                                            start=(m == 0), stop=(m == M - 1))
                last.then_inc(wo_ready, 1)

            attn_T(0)
            for tt in range(TT):
                if tt + 1 < TT:
                    attn_T(tt + 1)
                project(tt)
            pe.wait_ge(xn2_ready, TT)
            for u in range(4):
                c, half = u // 2, u % 2
                for i in range(4):
                    last = nc.tensor.transpose(bank[u][:, i * P:(i + 1) * P],
                                               xn[:, half * 4 + i, c * P:(c + 1) * P], ident[:])
                last.then_inc(xt2_ps, 1)
            pe.wait_ge(xt2_sb, 4)
            for tt in range(TT):
                for c in range(DC):
                    last = nc.tensor.matmul(bank[6][:, tt * E:(tt + 1) * E], xnT[:, c, tt * P:(tt + 1) * P],
                                            wg_sb[:, c, :], start=(c == 0), stop=(c == DC - 1))
            last.then_inc(logit_ps, 1)

            def expert_in(j):
                e, tb = j // 2, j % 2
                for ic in range(IC):
                    k = IC * j + ic
                    if k >= 4:
                        pe.wait_ge(h_ready, k - 3)
                    for c in range(DC):
                        last = nc.tensor.matmul(bank[k % 4][:], w1_sb[:, e, c, ic * P:(ic + 1) * P],
                                                xnT[:, c, tb * 512:(tb + 1) * 512], start=(c == 0), stop=(c == DC - 1))
                    last.then_inc(h_ps, 1)

            def expert_out(j):
                e, tb = j // 2, j % 2
                pe.wait_ge(h_ready, IC * (j + 1))
                for i in range(4):
                    k = 4 * j + i
                    if k >= 4:
                        pe.wait_ge(y_added, k - 3)
                    else:
                        pe.wait_ge(b2_added, TT)
                    for ic in range(IC):
                        last = nc.tensor.matmul(bank[4 + k % 4][:, 0:D], hT[:, j % 2, ic, i * P:(i + 1) * P],
                                                w2_sb[:, e, ic, :], start=(ic == 0), stop=(ic == IC - 1))
                    last.then_inc(y_ps, 1)

            expert_in(0)
            pe.wait_ge(onehot_ready, 1)
            for i in range(2):
                for t in range(4):
                    last = nc.tensor.transpose(bank[4 + i][0:E, t * P:(t + 1) * P], onehot[:, 4 * i + t, :], ident[:])
                last.then_inc(oht_ps, 1)
            pe.wait_ge(oht_sb, 2)
            for tt in range(TT):
                if tt >= 2:
                    pe.wait_ge(b2_added, tt - 1)
                nc.tensor.matmul(bank[6 + tt % 2][:, 0:D], onehotT[:, tt * P:(tt + 1) * P], b2_sb[:],
                                 start=True, stop=True).then_inc(b2_ps, 1)
            for j in range(2 * E):
                if j + 1 < 2 * E:
                    expert_in(j + 1)
                expert_out(j)


_INS = ['x', 'ctx_1024', 'mask_BxSxS2_bk1', 'g_xattn', 'g_ffn', 'L0_xattn_Wq', 'L0_xattn_Wk', 'L0_xattn_Wv',
        'L0_xattn_Wo', 'L0_xattn_bo', 'L0_ffn_Wg', 'L0_ffn_bg', 'L0_ffn_W1', 'L0_ffn_b1', 'L0_ffn_W2', 'L0_ffn_b2']


def kernel(**inputs):
    import numpy as _np
    import concourse.bacc as _bacc
    from concourse import mybir as _mybir
    from concourse.bass_utils import run_bass_kernel_spmd as _run

    nc = _bacc.Bacc("TRN2", target_bir_lowering=False, num_devices=1)
    arrays, args = {}, []
    for name in _INS:
        a = _np.ascontiguousarray(inputs[name])
        arrays[f"in_{name}_dram"] = a
        args.append(nc.dram_tensor(f"in_{name}_dram", a.shape, _mybir.dt.from_np(a.dtype), kind="ExternalInput").ap())
    shape = inputs['x'].shape
    args.append(nc.dram_tensor("out_0_dram", shape, _mybir.dt.float32, kind="ExternalOutput").ap())
    flamingo_kernel(nc, *args)
    r = _run(nc, [arrays], core_ids=[0])
    return r.results[0]["out_0_dram"]
```

```python
from contextlib import ExitStack

import concourse.bass as bass
from concourse import mybir

ALU = mybir.AluOpType
ACT = mybir.ActivationFunctionType
AX = mybir.AxisListType
F32 = mybir.dt.float32
BF16 = mybir.dt.bfloat16
I32 = mybir.dt.int32
U8 = mybir.dt.uint8
U16 = mybir.dt.uint16
F32R = mybir.dt.float32r
P = 128
EPS = 1e-5


def flamingo_kernel(nc, x, ctx_in, mask, g_xattn, g_ffn, wq, wk, wv, wo, bo, wg, bg, w1, b1, w2, b2, out):
    B, N, D = x.shape
    S = ctx_in.shape[1]
    INNER = wq.shape[1]
    DH = 64
    H = INNER // DH
    E, _, I = w1.shape
    SCALE = DH ** -0.5
    BIG = 3.3e38
    DC = D // P
    IC = I // P
    QT = N // P
    TT = B * QT
    T = B * N
    CK = 256
    KT = CK // P
    NC = S // CK
    M = INNER // P
    PER = 2 * M
    UNITS = 1 + M // 2 + KT * INNER // 512
    UNITS_ACT = 1 + M // 2 + 2
    UNITS_DVE = M // 2 + 2

    with ExitStack() as stack:
        def sb(name, shape, dt=F32):
            return stack.enter_context(nc.sbuf_tensor(name, shape, dt))

        def sem(name):
            return stack.enter_context(nc.semaphore(name))

        wq_sb = sb("wq_sb", [P, DC, INNER])
        wkv_sb = sb("wkv_sb", [P, 2, DC, INNER])
        wk_sb, wv_sb = wkv_sb[:, 0], wkv_sb[:, 1]
        wo_sb = sb("wo_sb", [P, M, D])
        w1_sb = wkv_sb[:].rearrange("p a c n -> p (a c n)").rearrange("p (e c i) -> p e c i", e=E, c=DC)
        wg_sb = sb("wg_sb", [P, DC, E])
        b1_sb = sb("b1_sb", [P, E, IC])
        b2_sb = sb("b2_sb", [E, D])
        bg_sb = sb("bg_sb", [P, E])
        bo_sb = sb("bo_sb", [P, D])
        gate_in = sb("gate_in", [P, 2])
        gate = sb("gate", [P, 2])
        x_sb = sb("x_sb", [P, TT, D])
        mask_sb = sb("mask_sb", [P, TT, S], U8)
        ident = sb("ident", [P, P])
        ident_bf = sb("ident_bf", [P, P], BF16)
        ones = sb("ones", [P, 1])
        stats = sb("stats", [P, TT, 6])
        mv = sb("mv", [P, TT, 2])
        std = sb("std", [P, TT])
        rstd = sb("rstd", [P, TT])
        eps = sb("eps", [P, 1])
        xnT = sb("xnT", [P, DC, T])
        q_hi = sb("q_hi", [P, M, N], F32R)
        q_lo = sb("q_lo", [P, M, N], F32R)
        rowmin = sb("rowmin", [P, TT, NC])
        fullrow = sb("fullrow", [P, TT])
        chunkmin = sb("chunkmin", [P, B, NC])
        fullb = sb("fullb", [P, B])
        visit_p = sb("visit_p", [P, B, NC])
        visit = sb("visit", [1, B * NC], I32)
        ctx_sb = sb("ctx_sb", [P, KT, D])
        k_hi = sb("k_hi", [P, M, 2, CK], F32R)
        k_lo = sb("k_lo", [P, M, 2, CK], F32R)
        v_sb = sb("v_sb", [P, KT, INNER])
        maskneg = sb("maskneg", [P, QT, CK], BF16)
        probs = sb("probs", [P, 2, 2, 2, CK])
        pT = sb("pT", [P, 2, 2, KT, CK])
        ctxT = pT[:, 0, 0]
        xn = pT[:].rearrange("p a h k n -> p (a h k n)").rearrange("p (t d) -> p t d", d=D)
        cmax = sb("cmax", [P, 2, 2, 2])
        negm = sb("negm", [P, QT, H])
        lsum = sb("lsum", [P, QT, H])
        r_col = sb("r_col", [P, 2, 2, 2])
        rinv = sb("rinv", [P, 2, 2, 2, DH])
        rinv_b = sb("rinv_b", [P, 2, CK])
        negm_run = sb("negm_run", [P, QT, H])
        l_run = sb("l_run", [P, QT, H])
        negm_new = sb("negm_new", [P, QT, H])
        w_old = sb("w_old", [P, QT, H])
        w_new = sb("w_new", [P, QT, H])
        w_wide = probs[:].rearrange("p a q h k -> p (a q h k)").rearrange("p (s a q h d) -> p s a q h d", s=2, a=2, q=QT, h=2)
        l_inv = sb("l_inv", [P, QT, H])
        oT = sb("oT", [P, B + 1, M, N])
        w2_sb = oT[:, B].rearrange("p m n -> p (m n)").rearrange("p (e c d) -> p e c d", e=E, c=IC)
        logits = sb("logits", [P, TT, E])
        lmax = sb("lmax", [P, TT])
        first_w = sb("first_w", [P, E])
        ismax = sb("ismax", [P, TT, E])
        onehot = sb("onehot", [P, TT, E])
        onehot_g = sb("onehot_g", [P, TT, E])
        onehotT = probs[:].rearrange("p a q h k -> p (a q h k)")[0:E, 0:T]
        hT = pT[:].rearrange("p a h k n -> p (a h k n)").rearrange("p (a c t) -> p a c t", a=2, c=IC)

        s_bank = [stack.enter_context(nc.psum_tensor(f"s_bank{i}", [P, 2, 512], F32)) for i in range(2)]
        one_bank = [stack.enter_context(nc.psum_tensor(f"bank{i}", [P, 512], F32)) for i in range(4)]
        bank = [s_bank[0][:, 0], s_bank[0][:, 1], s_bank[1][:, 0], s_bank[1][:, 1]] + [b[:] for b in one_bank]

        s_x = [sem(f"s_x{b}") for b in range(B)]
        s_wq = sem("s_wq")
        s_mask = [sem(f"s_mask{b}") for b in range(B)]
        s_wkv = sem("s_wkv")
        s_small = sem("s_small")
        s_ctx = sem("s_ctx")
        ident_ready = sem("ident_ready")
        pool_step = sem("pool_step")
        var_ready = sem("var_ready")
        std_ready = sem("std_ready")
        ln_ready = sem("ln_ready")
        dve_step = sem("dve_step")
        pro_ps = sem("pro_ps")
        pro_act = sem("pro_act")
        pro_dve = sem("pro_dve")
        visit_part = sem("visit_part")
        visit_ps = sem("visit_ps")
        visit_ready = sem("visit_ready")
        gate_ready = sem("gate_ready")
        xb_ready = sem("xb_ready")
        proj_ps = sem("proj_ps")
        proj_act = sem("proj_act")
        proj_dve = sem("proj_dve")
        mask_ready = sem("mask_ready")
        scores_ready = sem("scores_ready")
        cmax_done = sem("cmax_done")
        negm_ready = sem("negm_ready")
        probs_ready = sem("probs_ready")
        ptrans_ready = sem("ptrans_ready")
        pT_act = sem("pT_act")
        pT_dve = sem("pT_dve")
        r_col_ready = sem("r_col_ready")
        rinv_ready = sem("rinv_ready")
        rinv_ps = sem("rinv_ps")
        rinv_taken = sem("rinv_taken")
        o_ready = sem("o_ready")
        o_taken = sem("o_taken")
        merge_arg = sem("merge_arg")
        merge_exp = sem("merge_exp")
        merge_step = sem("merge_step")
        merge_w = sem("merge_w")
        merge_ps = sem("merge_ps")
        merged = sem("merged")
        attn_done = sem("attn_done")
        state_copied = sem("state_copied")
        s_wo = sem("s_wo")
        s_w1 = sem("s_w1")
        s_w2 = sem("s_w2")
        q_ps = sem("q_ps")
        q_hi_ready = sem("q_hi_ready")
        q_lo_ready = sem("q_lo_ready")
        zeroed = sem("zeroed")
        wo_ready = sem("wo_ready")
        x2_ready = sem("x2_ready")
        xn2_ready = sem("xn2_ready")
        xt2_ps = sem("xt2_ps")
        xt2_sb = sem("xt2_sb")
        logit_ps = sem("logit_ps")
        onehot_ready = sem("onehot_ready")
        oht_ps = sem("oht_ps")
        oht_sb = sem("oht_sb")
        b2_ps = sem("b2_ps")
        b2_added = sem("b2_added")
        h_ps = sem("h_ps")
        h_ready = sem("h_ready")
        y_ps = sem("y_ps")
        y_added = sem("y_added")
        s_out = sem("s_out")

        def chunk_dst(u):
            if u == 0:
                return ctxT.rearrange("p c k -> p (c k)")
            v = u - 1 - M // 2
            half = INNER // 512
            return v_sb[:, v // half, (v % half) * 512:(v % half + 1) * 512]

        def k_parts(k, u):
            for r in range(2):
                yield (k[r * DH:(r + 1) * DH, 2 * u - 2:2 * u, r, :],
                       bank[u % 4][r * DH:(r + 1) * DH, :].rearrange("p (m k) -> p m k", k=CK))

        block = stack.enter_context(nc.Block())

        @block.sync
        def _(sp):
            for b in range(B):
                sp.dma_start(x_sb[:, b * QT:(b + 1) * QT, :],
                             x[b].rearrange("(q p) d -> p q d", p=P)).then_inc(s_x[b], 16)
                sp.dma_start(mask_sb[:, b * QT:(b + 1) * QT, :],
                             mask[b].rearrange("(q p) k -> p q k", p=P)).then_inc(s_mask[b], 16)
                if b == 0:
                    sp.dma_start(wq_sb[:], wq.rearrange("(c p) n -> p c n", p=P)).then_inc(s_wq, 16)
            sp.dma_start(wk_sb, wk.rearrange("(c p) n -> p c n", p=P)).then_inc(s_wkv, 16)
            sp.dma_start(wv_sb, wv.rearrange("(c p) n -> p c n", p=P)).then_inc(s_wkv, 16)
            sp.dma_start(wo_sb[:], wo.rearrange("(m p) d -> p m d", p=P)).then_inc(s_wo, 16)
            sp.wait_ge(visit_ready, 1)
            done = sp.alloc_register("sp_done")
            sp.reg_mov(done, 0)
            for b in range(B):
                with sp.Fori(0, NC) as c:
                    flag = sp.value_load(visit[0:1, bass.ds(c + b * NC, 1)], min_val=0, max_val=1)
                    with sp.If(flag > 0):
                        n = sp.snap(done)
                        sp.wait_ge(proj_ps, n * UNITS + 1)
                        sp.dma_start(ctx_sb[:], ctx_in[b, bass.ds(c * CK, CK), :]
                                     .rearrange("(t p) d -> p t d", p=P)).then_inc(s_ctx, 16)
                        sp.reg_add(done, done, 1)
                    with sp.Else():
                        sp.nop()
            n = sp.snap(done)
            sp.wait_ge(proj_ps, n * UNITS + 1)
            sp.dma_start(w1_sb, w1.rearrange("e (c p) i -> p e c i", p=P)).then_inc(s_w1, 16)
            sp.wait_ge(attn_done, B)
            sp.dma_start(w2_sb, w2.rearrange("e (c p) d -> p e c d", p=P)).then_inc(s_w2, 16)
            for tt in range(TT):
                sp.wait_ge(y_added, (E - 1) * TT + tt + 1)
                b, q = tt // QT, tt % QT
                sp.dma_start(out[b, q * P:(q + 1) * P, :], x_sb[:, tt, :]).then_inc(s_out, 16)
            sp.wait_ge(s_out, 16 * TT)

        @block.gpsimd
        def _(pool):
            nc.gpsimd.memset(ident[:], 0.0).then_inc(pool_step, 1)
            nc.gpsimd.memset(ident_bf[:], 0.0).then_inc(pool_step, 1)
            nc.gpsimd.memset(eps[:], EPS).then_inc(ident_ready, 1)
            nc.gpsimd.memset(ones[:], 1.0).then_inc(ident_ready, 1)
            for e in range(E):
                nc.gpsimd.memset(first_w[:, e:e + 1], float(E - e)).then_inc(ident_ready, 1)
            pool.wait_ge(pool_step, 2)
            for m in (ident, ident_bf):
                nc.gpsimd.affine_select(out=m[:], in_=m[:], compare_op=ALU.not_equal, fill=1.0, base=0,
                                        pattern=[[-1, P]], channel_multiplier=1).then_inc(ident_ready, 1)
            for k in (k_hi, k_lo):
                nc.gpsimd.memset(k[:].bitcast(F32), 0.0).then_inc(zeroed, 1)
            pool.wait_ge(gate_ready, 1)
            pool.wait_ge(ln_ready, TT)
            nc.gpsimd.tensor_scalar(bo_sb[:], bo_sb[:], gate[:, 0:1], None, ALU.mult).then_inc(pool_step, 1)
            pool.wait_ge(pool_step, 3)
            nc.gpsimd.tensor_tensor(x_sb[:], x_sb[:], bo_sb[:].unsqueeze(1).broadcast_to([P, TT, D]),
                                    ALU.add).then_inc(xb_ready, 1)

        @block.scalar
        def _(act):
            act.dma_start(gate_in[:, 0:1], g_xattn.unsqueeze(0).broadcast_to([P, 1])).then_inc(s_small, 16)
            act.dma_start(gate_in[:, 1:2], g_ffn.unsqueeze(0).broadcast_to([P, 1])).then_inc(s_small, 16)
            act.dma_start(bo_sb[:], bo.unsqueeze(0).broadcast_to([P, D])).then_inc(s_small, 16)
            act.dma_start(bg_sb[:], bg.unsqueeze(0).broadcast_to([P, E])).then_inc(s_small, 16)
            act.dma_start(b1_sb[:], b1.rearrange("e (c p) -> p e c", p=P),
                          allow_slow_non_contiguous=True).then_inc(s_small, 16)
            act.dma_start(b2_sb[:], b2).then_inc(s_small, 16)
            act.dma_start(wg_sb[:], wg.rearrange("(c p) e -> p c e", p=P)).then_inc(s_small, 16)
            act.wait_ge(ident_ready, E + 4)
            for b in range(B):
                act.wait_ge(var_ready, b + 1)
                nc.scalar.activation(std[:, b * QT:(b + 1) * QT], mv[:, b * QT:(b + 1) * QT, 1], ACT.Sqrt,
                                     bias=eps[:]).then_inc(std_ready, 1)
            act.wait_ge(s_small, 16 * 7)
            nc.scalar.activation(gate[:], gate_in[:], ACT.Tanh).then_inc(gate_ready, 1)
            for u in range(0, 4, 2):
                act.wait_ge(pro_ps, u + 1)
                nc.scalar.copy(xnT[:, u // 2, (u % 2) * 512:(u % 2 + 1) * 512], bank[u]).then_inc(pro_act, 1)
            done = act.alloc_register("act_done")
            act.reg_mov(done, 0)
            merges = act.alloc_register("act_merges")
            act.reg_mov(merges, 0)
            later = act.alloc_register("act_later")
            for b in range(B):
                for m in range(M):
                    act.wait_ge(q_ps, b * M + m + 1)
                    nc.scalar.copy(q_hi[:, m, :], bank[m % 4]).then_inc(q_hi_ready, 1)
                act.reg_mov(later, 0)
                if b == 0:
                    act.wait_ge(visit_ready, 1)
                    act.wait_ge(zeroed, 2)
                with act.Fori(0, NC) as c:
                    flag = act.value_load(visit[0:1, bass.ds(c + b * NC, 1)], min_val=0, max_val=1)
                    with act.If(flag > 0):
                        n = act.snap(done)
                        units = n * UNITS
                        g = n * PER
                        act.wait_ge(proj_ps, units + 2)
                        nc.scalar.copy(chunk_dst(0), bank[0]).then_inc(proj_act, 1)
                        for u in range(1, 1 + M // 2):
                            act.wait_ge(proj_ps, units + (u + 2))
                            for dst, src in k_parts(k_hi, u):
                                last = nc.scalar.copy(dst, src)
                            last.then_inc(proj_act, 1)
                        for u in range(1 + M // 2, UNITS, 2):
                            act.wait_ge(proj_ps, units + (u + 2))
                            nc.scalar.copy(chunk_dst(u), bank[u % 4]).then_inc(proj_act, 1)

                        def take_pT(u):
                            act.wait_ge(ptrans_ready, g * 2 + (2 * u + 1))
                            act.wait_ge(o_ready, g + (max(u - 1, 0) + 1))
                            nc.scalar.copy(pT[:, u % 2, 0].rearrange("p t n -> p (t n)"), bank[4]).then_inc(pT_act, 1)

                        def take_rinv(u):
                            act.wait_ge(rinv_ps, g + (u + 1))
                            act.wait_ge(o_taken, g + (max(u - 1, 0) + 1))
                            nc.scalar.copy(rinv_b[:, u % 2, :], bank[7][:, 0:CK]).then_inc(rinv_taken, 1)

                        for u in range(PER):
                            m, j = u // 2, u % 2
                            act.wait_ge(negm_ready, g + (u + 1))
                            for i in range(2):
                                if i == 1 and u >= 1:
                                    take_pT(u - 1)
                                if i == 0 and u >= 2:
                                    act.wait_ge(ptrans_ready, g * 2 + 2 * (u - 1))
                                for h in range(2):
                                    col = negm[:, 2 * j + i, 2 * m + h:2 * m + h + 1]
                                    last = nc.scalar.activation(probs[:, u % 2, i, h, :],
                                                                s_bank[u % 2][:, i, h * CK:(h + 1) * CK], ACT.Exp,
                                                                bias=col, scale=SCALE,
                                                                accum_out=lsum[:, 2 * j + i, 2 * m + h:2 * m + h + 1])
                            last.then_inc(probs_ready, 1)
                            if u >= 1:
                                take_rinv(u - 1)
                        take_pT(PER - 1)
                        take_rinv(PER - 1)
                        act.reg_add(done, done, 1)
                        with act.If(act.snap(later) > 0):
                            k = act.snap(merges)
                            act.wait_ge(merge_arg, k + 1)
                            nc.scalar.activation(w_old[:], w_old[:], ACT.Exp)
                            nc.scalar.activation(w_new[:], w_new[:], ACT.Exp).then_inc(merge_exp, 1)
                            act.reg_add(merges, merges, 1)
                        with act.Else():
                            act.nop()
                        act.reg_mov(later, 1)
                    with act.Else():
                        act.nop()
            act.wait_ge(var_ready, B + 1)
            nc.scalar.activation(std[:], mv[:, :, 1], ACT.Sqrt, bias=eps[:]).then_inc(std_ready, 1)
            for u in range(4):
                act.wait_ge(xt2_ps, u + 1)
                nc.scalar.copy(xnT[:, u // 2, (u % 2) * 512:(u % 2 + 1) * 512], bank[u % 4]).then_inc(xt2_sb, 1)
            k = 0
            for e in range(E):
                for tb in range(T // 512):
                    for ic in range(IC):
                        act.wait_ge(h_ps, k + 1)
                        if k >= 2 * IC:
                            act.wait_ge(y_ps, ((k // IC) - 1) * 4)
                        nc.scalar.activation(hT[:, (k // IC) % 2, ic, :], bank[k % 4], ACT.Gelu,
                                             bias=b1_sb[:, e, ic:ic + 1]).then_inc(h_ready, 1)
                        k += 1

        @block.vector
        def _(dve):
            steps, stds = [0], [0]
            dve.sem_inc(o_taken, 1)

            def then(ins):
                steps[0] += 1
                ins.then_inc(dve_step, 1)
                dve.wait_ge(dve_step, steps[0])

            def variance(tiles):
                for t in tiles:
                    last = nc.vector.bn_stats(stats[:, t, :], x_sb[:, t, :])
                then(last)
                for t in tiles:
                    last = nc.vector.bn_aggr(mv[:, t, :], stats[:, t, :])
                return last

            def norm(a, z, ready):
                stds[0] += 1
                dve.wait_ge(std_ready, stds[0])
                then(nc.vector.reciprocal(rstd[:, a:z], std[:, a:z]))
                for t in range(a, z):
                    nc.vector.tensor_scalar(xn[:, t, :], x_sb[:, t, :], mv[:, t, 0:1], rstd[:, t:t + 1],
                                            ALU.subtract, ALU.mult).then_inc(ready, 1)

            def take_q(b, m):
                dve.wait_ge(q_hi_ready, b * M + m + 1)
                nc.vector.tensor_tensor(q_lo[:, m, :], bank[m % 4], q_hi[:, m, :].bitcast(F32),
                                        ALU.subtract).then_inc(q_lo_ready, 1)

            for b in range(B):
                dve.wait_ge(s_x[b], 16)
                variance(range(b * QT, (b + 1) * QT)).then_inc(var_ready, 1)
                norm(b * QT, (b + 1) * QT, ln_ready)
            for u in range(1, 4, 2):
                dve.wait_ge(pro_ps, u + 1)
                nc.vector.tensor_copy(xnT[:, u // 2, (u % 2) * 512:(u % 2 + 1) * 512], bank[u]).then_inc(pro_dve, 1)
            for t in range(0, TT, 2):
                dve.wait_ge(s_mask[t // QT], 16)
                pairs = mask_sb[:, t:t + 2, :].rearrange("p t k -> p (t k)").bitcast(U16)
                last = nc.vector.tensor_reduce(rowmin[:, t:t + 2, :].rearrange("p t c -> p (t c)"),
                                               pairs.rearrange("p (n k) -> p n k", k=CK // 2), AX.X, ALU.min)
                take_q(0, t // 2)
            then(last)
            then(nc.vector.tensor_scalar(rowmin[:], rowmin[:], 257.0, None, ALU.is_ge))
            nc.vector.tensor_reduce(chunkmin[:], rowmin[:].rearrange("p (b q) c -> p b c q", b=B), AX.X, ALU.min)
            then(nc.vector.tensor_reduce(fullrow[:], rowmin[:], AX.X, ALU.min))
            then(nc.vector.tensor_reduce(fullb[:], fullrow[:].rearrange("p (b q) -> p b q", b=B), AX.X, ALU.max))
            nc.vector.tensor_tensor(visit_p[:], fullb[:].unsqueeze(2).broadcast_to([P, B, NC]), chunkmin[:],
                                    ALU.subtract).then_inc(visit_part, 1)
            dve.wait_ge(visit_ps, 1)
            nc.vector.tensor_scalar(visit[:], bank[4][0:1, 0:B * NC], -P + 0.5, None, ALU.is_gt)\
                .then_inc(visit_ready, 1)
            done = dve.alloc_register("dve_done")
            dve.reg_mov(done, 0)
            merges = dve.alloc_register("dve_merges")
            dve.reg_mov(merges, 0)
            later = dve.alloc_register("dve_later")
            for b in range(B):
                for m in range(4 if b == 0 else 0, M):
                    take_q(b, m)
                dve.reg_mov(later, 0)
                if b == 0:
                    dve.wait_ge(visit_ready, 1)
                    dve.wait_ge(zeroed, 2)
                with dve.Fori(0, NC) as c:
                    flag = dve.value_load(visit[0:1, bass.ds(c + b * NC, 1)], min_val=0, max_val=1)
                    with dve.If(flag > 0):
                        n = dve.snap(done)
                        slot = dve.snap(dve.snap(later, min_val=0, max_val=1) * (B - b) + b, min_val=0, max_val=B)
                        units = n * UNITS
                        g = n * PER
                        dve.wait_ge(scores_ready, g + 1)
                        nc.vector.tensor_scalar(maskneg[:], mask_sb[:, b * QT:(b + 1) * QT, bass.ds(c * CK, CK)],
                                                -BIG, None, ALU.mult).then_inc(mask_ready, 1)
                        for u in range(1, 1 + M // 2):
                            dve.wait_ge(proj_act, n * UNITS_ACT + (u + 1))
                            for (dst, src), (hi, _) in zip(k_parts(k_lo, u), k_parts(k_hi, u)):
                                last = nc.vector.tensor_tensor(dst, src, hi.bitcast(F32), ALU.subtract)
                            last.then_inc(proj_dve, 1)
                        for u in range(2 + M // 2, UNITS, 2):
                            dve.wait_ge(proj_ps, units + (u + 2))
                            nc.vector.tensor_copy(chunk_dst(u), bank[u % 4]).then_inc(proj_dve, 1)

                        def take_max(u):
                            m, j = u // 2, u % 2
                            dve.wait_ge(scores_ready, g + (u + 2))
                            nc.vector.tensor_reduce(cmax[:, u % 2], s_bank[u % 2][:].rearrange("p i (h k) -> p i h k", h=2),
                                                    AX.X, ALU.max).then_inc(cmax_done, 1)
                            dve.wait_ge(cmax_done, g + (u + 1))
                            nc.vector.tensor_scalar(negm[:, 2 * j:2 * j + 2, 2 * m:2 * m + 2], cmax[:, u % 2], -SCALE,
                                                    None, ALU.mult).then_inc(negm_ready, 1)

                        def take_sum(u):
                            m, j = u // 2, u % 2
                            dve.wait_ge(probs_ready, g + (u + 1))
                            nc.vector.reciprocal(r_col[:, u % 2], lsum[:, 2 * j:2 * j + 2, 2 * m:2 * m + 2])\
                                .then_inc(r_col_ready, 1)
                            dve.wait_ge(r_col_ready, g + (u + 1))
                            nc.vector.tensor_copy(rinv[:, u % 2], r_col[:, u % 2].unsqueeze(3)
                                                  .broadcast_to([P, 2, 2, DH]))\
                                .then_inc(rinv_ready, 1)

                        def take_pT(u):
                            dve.wait_ge(ptrans_ready, g * 2 + (2 * u + 2))
                            dve.wait_ge(o_ready, g + (max(u - 1, 0) + 1))
                            nc.vector.tensor_copy(pT[:, u % 2, 1].rearrange("p t n -> p (t n)"), bank[5]).then_inc(pT_dve, 1)

                        def take_o(u):
                            m, j = u // 2, u % 2
                            dve.wait_ge(o_ready, g + (u + 2))
                            dve.wait_ge(rinv_taken, g + (u + 1))
                            dst = oT[:].rearrange("p s m n -> p s (m n)")[:, bass.ds(slot, 1), m * N + j * CK:m * N + (j + 1) * CK]
                            nc.vector.tensor_tensor(dst.rearrange("p s n -> p (s n)"), bank[6][:, 0:CK], rinv_b[:, u % 2, :],
                                                    ALU.mult).then_inc(o_taken, 1)

                        take_max(0)
                        for u in range(PER):
                            if u + 1 < PER:
                                take_max(u + 1)
                            take_sum(u)
                            take_pT(u)
                            if u >= 1:
                                take_o(u - 1)
                        take_o(PER - 1)
                        dve.reg_add(done, done, 1)
                        with dve.If(dve.snap(later) > 0):
                            k = dve.snap(merges)
                            ks = k * 6
                            nc.vector.tensor_tensor(negm_new[:], negm_run[:], negm[:], ALU.min).then_inc(merge_step, 1)
                            dve.wait_ge(merge_step, ks + 1)
                            nc.vector.tensor_tensor(w_old[:], negm_new[:], negm_run[:], ALU.subtract)
                            nc.vector.tensor_tensor(w_new[:], negm_new[:], negm[:], ALU.subtract).then_inc(merge_arg, 1)
                            dve.wait_ge(merge_exp, k + 1)
                            nc.vector.tensor_copy(negm_run[:], negm_new[:])
                            nc.vector.tensor_tensor(w_old[:], w_old[:], l_run[:], ALU.mult)
                            nc.vector.tensor_tensor(w_new[:], w_new[:], lsum[:], ALU.mult).then_inc(merge_step, 1)
                            dve.wait_ge(merge_step, ks + 2)
                            nc.vector.tensor_tensor(l_run[:], w_old[:], w_new[:], ALU.add).then_inc(merge_step, 1)
                            dve.wait_ge(merge_step, ks + 3)
                            nc.vector.reciprocal(l_inv[:], l_run[:]).then_inc(merge_step, 1)
                            dve.wait_ge(merge_step, ks + 4)
                            nc.vector.tensor_tensor(w_old[:], w_old[:], l_inv[:], ALU.mult)
                            nc.vector.tensor_tensor(w_new[:], w_new[:], l_inv[:], ALU.mult).then_inc(merge_step, 1)
                            dve.wait_ge(merge_step, ks + 5)

                            def widen(m):
                                for a, w in enumerate((w_old, w_new)):
                                    last = nc.vector.tensor_copy(w_wide[:, m % 2, a], w[:, :, 2 * m:2 * m + 2]
                                                                 .unsqueeze(3).broadcast_to([P, QT, 2, DH]))
                                last.then_inc(merge_w, 1)

                            widen(0)
                            for m in range(M):
                                if m + 1 < M:
                                    if m >= 1:
                                        dve.wait_ge(merge_ps, k * M + m)
                                    widen(m + 1)
                                dve.wait_ge(merge_ps, k * M + (m + 1))
                                nc.vector.tensor_tensor(oT[:, b, m, :], oT[:, b, m, :], s_bank[m % 2][:, 0], ALU.mult)
                                nc.vector.tensor_tensor(oT[:, B, m, :], oT[:, B, m, :], s_bank[m % 2][:, 1], ALU.mult)\
                                    .then_inc(merged, 1)
                                dve.wait_ge(merged, k * M + (m + 1))
                                last = nc.vector.tensor_tensor(oT[:, b, m, :], oT[:, b, m, :], oT[:, B, m, :], ALU.add)
                            last.then_inc(merge_step, 1)
                            dve.wait_ge(merge_step, ks + 6)
                            dve.reg_add(merges, merges, 1)
                        with dve.Else():
                            nc.vector.tensor_copy(negm_run[:], negm[:])
                            nc.vector.tensor_copy(l_run[:], lsum[:]).then_inc(state_copied, 1)
                            dve.wait_ge(state_copied, b + 1)
                        dve.reg_mov(later, 1)
                    with dve.Else():
                        dve.nop()
                nc.vector.memset(cmax[:], 0.0).then_inc(attn_done, 1)
                if b == 0:
                    dve.wait_ge(xb_ready, 1)
                for q in range(QT):
                    tt = b * QT + q
                    dve.wait_ge(wo_ready, tt + 1)
                    nc.vector.scalar_tensor_tensor(x_sb[:, tt, :], bank[6 + tt % 2][:, 0:D], gate[:, 0:1], x_sb[:, tt, :],
                                                   ALU.mult, ALU.add).then_inc(x2_ready, 1)
                dve.wait_ge(x2_ready, (b + 1) * QT)
                last = variance(range(b * QT, (b + 1) * QT))
            last.then_inc(var_ready, 1)
            norm(0, TT, xn2_ready)
            dve.wait_ge(logit_ps, 1)
            then(nc.vector.tensor_tensor(logits[:], bank[6][:, 0:TT * E].rearrange("p (t e) -> p t e", e=E),
                                         bg_sb[:].unsqueeze(1).broadcast_to([P, TT, E]), ALU.add))
            then(nc.vector.tensor_reduce(lmax[:], logits[:], AX.X, ALU.max))
            then(nc.vector.tensor_tensor(ismax[:], logits[:], lmax[:].unsqueeze(2).broadcast_to([P, TT, E]),
                                         ALU.is_equal))
            then(nc.vector.tensor_tensor(ismax[:], ismax[:], first_w[:].unsqueeze(1).broadcast_to([P, TT, E]),
                                         ALU.mult))
            then(nc.vector.tensor_reduce(lmax[:], ismax[:], AX.X, ALU.max))
            nc.vector.tensor_tensor(onehot[:], ismax[:], lmax[:].unsqueeze(2).broadcast_to([P, TT, E]),
                                    ALU.is_equal).then_inc(onehot_ready, 1)
            dve.wait_ge(onehot_ready, 1)
            then(nc.vector.tensor_scalar(onehot_g[:], onehot[:], gate[:, 1:2], None, ALU.mult))
            for i in range(2):
                dve.wait_ge(oht_ps, i + 1)
                nc.vector.tensor_copy(onehotT[:, i * 512:(i + 1) * 512], bank[4 + i][0:E, :]).then_inc(oht_sb, 1)
            for tt in range(TT):
                dve.wait_ge(b2_ps, tt + 1)
                nc.vector.scalar_tensor_tensor(x_sb[:, tt, :], bank[6 + tt % 2][:, 0:D], gate[:, 1:2], x_sb[:, tt, :],
                                               ALU.mult, ALU.add).then_inc(b2_added, 1)
            k = 0
            for e in range(E):
                for tt in range(TT):
                    dve.wait_ge(y_ps, k + 1)
                    if e == 0:
                        dve.wait_ge(b2_added, TT)
                    else:
                        dve.wait_ge(y_added, k - TT + 1)
                    nc.vector.scalar_tensor_tensor(x_sb[:, tt, :], bank[4 + k % 4][:, 0:D], onehot_g[:, tt, e:e + 1],
                                                   x_sb[:, tt, :], ALU.mult, ALU.add).then_inc(y_added, 1)
                    k += 1

        @block.tensor
        def _(pe):
            pe.sem_inc(proj_ps, 1)
            pe.sem_inc(scores_ready, 1)
            pe.sem_inc(o_ready, 1)
            pe.wait_ge(ident_ready, E + 4)
            for u in range(4):
                c, half = u // 2, u % 2
                pe.wait_ge(ln_ready, 4 * (half + 1))
                for i in range(4):
                    last = nc.tensor.transpose(bank[u][:, i * P:(i + 1) * P],
                                               xn[:, half * 4 + i, c * P:(c + 1) * P], ident[:])
                last.then_inc(pro_ps, 1)
            pe.wait_ge(pro_act, 2)
            pe.wait_ge(pro_dve, 2)
            pe.wait_ge(s_wq, 16)
            done = pe.alloc_register("pe_done")
            pe.reg_mov(done, 0)
            merges = pe.alloc_register("pe_merges")
            pe.reg_mov(merges, 0)
            later = pe.alloc_register("pe_later")
            for b in range(B):
                for m in range(M):
                    if m >= 4:
                        pe.wait_ge(q_lo_ready, b * M + m - 3)
                    for c in range(DC):
                        last = nc.tensor.matmul(bank[m % 4], wq_sb[:, c, m * P:(m + 1) * P],
                                                xnT[:, c, b * N:(b + 1) * N], start=(c == 0), stop=(c == DC - 1))
                    last.then_inc(q_ps, 1)
                if b == 0:
                    pe.wait_ge(visit_part, 1)
                    nc.tensor.matmul(bank[4][0:1, 0:B * NC], ones[:], visit_p[:].rearrange("p b c -> p (b c)"),
                                     start=True, stop=True).then_inc(visit_ps, 1)
                    pe.wait_ge(visit_ready, 1)
                    pe.wait_ge(s_wkv, 32)
                pe.wait_ge(q_lo_ready, (b + 1) * M)
                pe.reg_mov(later, 0)
                with pe.Fori(0, NC) as cc:
                    flag = pe.value_load(visit[0:1, bass.ds(cc + b * NC, 1)], min_val=0, max_val=1)
                    with pe.If(flag > 0):
                        n = pe.snap(done)
                        g = n * PER
                        ua, ud = n * UNITS_ACT, n * UNITS_DVE
                        pe.wait_ge(s_ctx, n * 16 + 16)
                        for c in range(DC):
                            for t in range(KT):
                                last = nc.tensor.transpose(bank[0][:, c * CK + t * P:c * CK + (t + 1) * P],
                                                           ctx_sb[:, t, c * P:(c + 1) * P], ident[:])
                        last.then_inc(proj_ps, 1)
                        pe.wait_ge(proj_act, ua + 1)
                        for u in range(1, UNITS):
                            if u >= 5:
                                pe.wait_ge(proj_dve, ud + (u - 4))
                            if u <= M // 2:
                                for i in range(2):
                                    m = 2 * (u - 1) + i
                                    for c in range(DC):
                                        last = nc.tensor.matmul(bank[u % 4][:, i * CK:(i + 1) * CK],
                                                                wk_sb[:, c, m * P:(m + 1) * P], ctxT[:, c, :],
                                                                start=(c == 0), stop=(c == DC - 1))
                            else:
                                v = u - 1 - M // 2
                                t, half = v // (INNER // 512), v % (INNER // 512)
                                for c in range(DC):
                                    last = nc.tensor.matmul(bank[u % 4], ctxT[:, c, t * P:(t + 1) * P],
                                                            wv_sb[:, c, half * 512:(half + 1) * 512],
                                                            start=(c == 0), stop=(c == DC - 1))
                            last.then_inc(proj_ps, 1)
                        pe.wait_ge(proj_act, ua + UNITS_ACT)
                        pe.wait_ge(proj_dve, ud + UNITS_DVE)
                        pe.wait_ge(mask_ready, n + 1)

                        def scores(u):
                            if u >= 2:
                                pe.wait_ge(probs_ready, g + (u - 1))
                            m, j = u // 2, u % 2
                            for i in range(2):
                                q = 2 * j + i
                                s = s_bank[u % 2][:, i, :]
                                for n_, (a, k) in enumerate(((q_lo, k_hi), (q_hi, k_lo), (q_hi, k_hi))):
                                    nc.tensor.matmul(s, a[:, m, q * P:(q + 1) * P], k[:, m].rearrange("p h k -> p (h k)"),
                                                     start=(n_ == 0), stop=False)
                                last = nc.tensor.matmul(s.rearrange("p (h k) -> p h k", h=2), ident_bf[:],
                                                        maskneg[:, q, :].unsqueeze(1).broadcast_to([P, 2, CK]),
                                                        start=False, stop=True)
                            last.then_inc(scores_ready, 1)

                        def transposes(u):
                            pe.wait_ge(probs_ready, g + (u + 1))
                            if u >= 1:
                                pe.wait_ge(pT_act, g + u)
                                pe.wait_ge(pT_dve, g + u)
                            for h in range(2):
                                for t in range(KT):
                                    for i in range(2):
                                        last = nc.tensor.transpose(bank[4 + h][:, t * CK + i * P:t * CK + (i + 1) * P],
                                                                   probs[:, u % 2, i, h, t * P:(t + 1) * P], ident[:])
                                last.then_inc(ptrans_ready, 1)

                        def values(u):
                            m = u // 2
                            pe.wait_ge(rinv_ready, g + (u + 1))
                            if u >= 1:
                                pe.wait_ge(rinv_taken, g + u)
                            else:
                                pe.wait_ge(o_taken, g + 1)
                            for i in range(2):
                                last = nc.tensor.transpose(bank[7][:, i * P:(i + 1) * P], rinv[:, u % 2, i].rearrange("p h d -> p (h d)"), ident[:])
                            last.then_inc(rinv_ps, 1)
                            pe.wait_ge(pT_act, g + (u + 1))
                            pe.wait_ge(pT_dve, g + (u + 1))
                            pe.wait_ge(o_taken, g + (u + 1))
                            for t in range(KT):
                                for h in range(2):
                                    last = nc.tensor.matmul(bank[6][h * DH:(h + 1) * DH, 0:CK],
                                                            v_sb[:, t, (2 * m + h) * DH:(2 * m + h + 1) * DH],
                                                            pT[:, u % 2, h, t, :], start=(t == 0), stop=(t == KT - 1))
                            last.then_inc(o_ready, 1)

                        scores(0)
                        for u in range(PER):
                            if u + 1 < PER:
                                scores(u + 1)
                            if u >= 1:
                                values(u - 1)
                            transposes(u)
                        values(PER - 1)
                        pe.reg_add(done, done, 1)
                        with pe.If(pe.snap(later) > 0):
                            k = pe.snap(merges)
                            for m in range(M):
                                pe.wait_ge(merge_w, k * M + (m + 1))
                                if m >= 2:
                                    pe.wait_ge(merged, k * M + (m - 1))
                                for a in range(2):
                                    for q in range(QT):
                                        last = nc.tensor.transpose(s_bank[m % 2][:, a, q * P:(q + 1) * P],
                                                                   w_wide[:, m % 2, a, q].rearrange("p h d -> p (h d)"), ident[:])
                                last.then_inc(merge_ps, 1)
                            pe.wait_ge(merged, k * M + M)
                            pe.reg_add(merges, merges, 1)
                        with pe.Else():
                            pe.nop()
                        pe.reg_mov(later, 1)
                    with pe.Else():
                        pe.nop()
                if b == 0:
                    pe.wait_ge(s_wo, 16)
                pe.wait_ge(attn_done, b + 1)
                for q in range(QT):
                    tt = b * QT + q
                    if q >= 2:
                        pe.wait_ge(x2_ready, tt - 1)
                    for m in range(M):
                        last = nc.tensor.matmul(bank[6 + tt % 2][:, 0:D], oT[:, b, m, q * P:(q + 1) * P], wo_sb[:, m, :],
                                                start=(m == 0), stop=(m == M - 1))
                    last.then_inc(wo_ready, 1)
                pe.wait_ge(x2_ready, (b + 1) * QT)
            pe.wait_ge(s_w1, 16)
            pe.wait_ge(xn2_ready, TT)
            for u in range(4):
                c, half = u // 2, u % 2
                for i in range(4):
                    last = nc.tensor.transpose(bank[u][:, i * P:(i + 1) * P],
                                               xn[:, half * 4 + i, c * P:(c + 1) * P], ident[:])
                last.then_inc(xt2_ps, 1)
            pe.wait_ge(xt2_sb, 4)
            for tt in range(TT):
                for c in range(DC):
                    last = nc.tensor.matmul(bank[6][:, tt * E:(tt + 1) * E], xnT[:, c, tt * P:(tt + 1) * P],
                                            wg_sb[:, c, :], start=(c == 0), stop=(c == DC - 1))
            last.then_inc(logit_ps, 1)

            def expert_in(j):
                e, tb = j // 2, j % 2
                for ic in range(IC):
                    k = IC * j + ic
                    if k >= 4:
                        pe.wait_ge(h_ready, k - 3)
                    for c in range(DC):
                        last = nc.tensor.matmul(bank[k % 4], w1_sb[:, e, c, ic * P:(ic + 1) * P],
                                                xnT[:, c, tb * 512:(tb + 1) * 512], start=(c == 0), stop=(c == DC - 1))
                    last.then_inc(h_ps, 1)

            def expert_out(j):
                e, tb = j // 2, j % 2
                pe.wait_ge(h_ready, IC * (j + 1))
                for i in range(4):
                    k = 4 * j + i
                    if k >= 4:
                        pe.wait_ge(y_added, k - 3)
                    else:
                        pe.wait_ge(b2_added, TT)
                    for ic in range(IC):
                        last = nc.tensor.matmul(bank[4 + k % 4][:, 0:D], hT[:, j % 2, ic, i * P:(i + 1) * P],
                                                w2_sb[:, e, ic, :], start=(ic == 0), stop=(ic == IC - 1))
                    last.then_inc(y_ps, 1)

            expert_in(0)
            pe.wait_ge(s_w2, 16)
            pe.wait_ge(onehot_ready, 1)
            for i in range(2):
                for t in range(4):
                    last = nc.tensor.transpose(bank[4 + i][0:E, t * P:(t + 1) * P], onehot[:, 4 * i + t, :], ident[:])
                last.then_inc(oht_ps, 1)
            pe.wait_ge(oht_sb, 2)
            for tt in range(TT):
                if tt >= 2:
                    pe.wait_ge(b2_added, tt - 1)
                nc.tensor.matmul(bank[6 + tt % 2][:, 0:D], onehotT[:, tt * P:(tt + 1) * P], b2_sb[:],
                                 start=True, stop=True).then_inc(b2_ps, 1)
            for j in range(2 * E):
                if j + 1 < 2 * E:
                    expert_in(j + 1)
                expert_out(j)


_INS = ['x', 'ctx_1024', 'mask_BxSxS2_bk1', 'g_xattn', 'g_ffn', 'L0_xattn_Wq', 'L0_xattn_Wk', 'L0_xattn_Wv',
        'L0_xattn_Wo', 'L0_xattn_bo', 'L0_ffn_Wg', 'L0_ffn_bg', 'L0_ffn_W1', 'L0_ffn_b1', 'L0_ffn_W2', 'L0_ffn_b2']


def kernel(**inputs):
    import numpy as _np
    import concourse.bacc as _bacc
    from concourse import mybir as _mybir
    from concourse.bass_utils import run_bass_kernel_spmd as _run

    nc = _bacc.Bacc("TRN2", target_bir_lowering=False, num_devices=1)
    arrays, args = {}, []
    for name in _INS:
        a = _np.ascontiguousarray(inputs[name])
        arrays[f"in_{name}_dram"] = a
        args.append(nc.dram_tensor(f"in_{name}_dram", a.shape, _mybir.dt.from_np(a.dtype), kind="ExternalInput").ap())
    shape = inputs['x'].shape
    args.append(nc.dram_tensor("out_0_dram", shape, _mybir.dt.float32, kind="ExternalOutput").ap())
    flamingo_kernel(nc, *args)
    r = _run(nc, [arrays], core_ids=[0])
    return r.results[0]["out_0_dram"]
```

```python
from contextlib import ExitStack
import math

import concourse.bass as bass
from concourse import mybir

ALU = mybir.AluOpType
ACT = mybir.ActivationFunctionType
AX = mybir.AxisListType
F32 = mybir.dt.float32
BF16 = mybir.dt.bfloat16
I32 = mybir.dt.int32
U8 = mybir.dt.uint8
U16 = mybir.dt.uint16
F32R = mybir.dt.float32r
P = 128
EPS = 1e-5


def flamingo_kernel(nc, x, ctx_in, mask, g_xattn, g_ffn, wq, wk, wv, wo, bo, wg, bg, w1, b1, w2, b2, out):
    B, N, D = x.shape
    S = ctx_in.shape[1]
    INNER = wq.shape[1]
    DH = 64
    H = INNER // DH
    E, _, I = w1.shape
    SCALE = DH ** -0.5
    BIG = 3.3e38
    DC = D // P
    IC = I // P
    QT = N // P
    TT = B * QT
    T = B * N
    CK = 256
    KT = CK // P
    NC = S // CK
    M = INNER // P
    PER = 2 * M
    UNITS = 1 + M // 2 + KT * INNER // 512
    UNITS_ACT = 1 + M // 2 + 2
    UNITS_DVE = M // 2 + 2
    NT = TT + E
    RW = D + 4
    MEAN, VAR, RSTD, TOKEN = D, D + 1, D + 2, D + 3
    NOWHERE = T
    sorted_rows = nc.dram_tensor("sorted_rows", [NT * P, RW], F32, kind="Internal").ap()

    with ExitStack() as stack:
        def sb(name, shape, dt=F32):
            return stack.enter_context(nc.sbuf_tensor(name, shape, dt))

        def sem(name):
            return stack.enter_context(nc.semaphore(name))

        wq_sb = sb("wq_sb", [P, DC, INNER])
        wkv_sb = sb("wkv_sb", [P, 2, DC, INNER])
        wk_sb, wv_sb = wkv_sb[:, 0], wkv_sb[:, 1]
        wo_sb = sb("wo_sb", [P, M, D])
        w1_sb = wkv_sb[:].rearrange("p a c n -> p (a c n)").rearrange("p (e c i) -> p e c i", e=E, c=DC)
        wg_sb = sb("wg_sb", [P, DC, E])
        bg_sb = sb("bg_sb", [P, E])
        bo_sb = sb("bo_sb", [P, D])
        gate_in = sb("gate_in", [P, 2])
        gate = sb("gate", [P, 2])
        rows = sb("rows", [P, TT, RW])
        x_sb = rows[:, :, 0:D]
        mask_sb = sb("mask_sb", [P, TT, S], U8)
        ident = sb("ident", [P, P])
        ident_bf = sb("ident_bf", [P, P], BF16)
        ones = sb("ones", [P, P])
        before = sb("before", [P, P])
        e_before = sb("e_before", [P, E, E])
        tile_start = sb("tile_start", [P, TT])
        tile_no = sb("tile_no", [1, NT + 2])
        empty_row = sb("empty_row", [P, RW])
        stats = sb("stats", [P, TT, 6])
        std = sb("std", [P, TT])
        eps = sb("eps", [P, 1])
        warm = sb("warm", [P, 1])
        xnT = sb("xnT", [P, DC, T])
        q_parts = sb("q_parts", [P, M, 2, N], F32R)
        rowmin = sb("rowmin", [P, TT, NC])
        fullrow = sb("fullrow", [P, TT])
        chunkmin = sb("chunkmin", [P, B, NC])
        fullb = sb("fullb", [P, B])
        visit_p = sb("visit_p", [P, B, NC])
        visited = sb("visited", [1, NC])
        visit_cmp = sb("visit_cmp", [1, NC + 1, NC])
        visit_cum = sb("visit_cum", [1, NC])
        visit_no = sb("visit_no", [1, NC + 1])
        visit = sb("visit", [1, B * (NC + 2)], I32)
        ctx_sb = sb("ctx_sb", [P, KT, D])
        k_hi = sb("k_hi", [P, M, 2, CK], F32R)
        k_lo = sb("k_lo", [P, M, 2, CK], F32R)
        v_sb = sb("v_sb", [P, KT, INNER])
        maskneg = sb("maskneg", [P, QT, CK], BF16)
        probs = sb("probs", [P, 2, 2, 2, CK])
        pT = sb("pT", [P, 2, 2, KT, CK])
        ctxT = pT[:, 0, 0]
        xn = pT[:].rearrange("p a h k n -> p (a h k n)").rearrange("p (t d) -> p t d", d=D)
        cmax = sb("cmax", [P, 2, 2, 2])
        negm = sb("negm", [P, QT, H])
        lsum = sb("lsum", [P, QT, H])
        r_col = sb("r_col", [P, 2, 2, 2])
        rinv = sb("rinv", [P, 2, 2, 2, DH])
        rinv_b = sb("rinv_b", [P, 2, CK])
        negm_run = sb("negm_run", [P, QT, H])
        l_run = sb("l_run", [P, QT, H])
        negm_new = sb("negm_new", [P, QT, H])
        w_old = sb("w_old", [P, QT, H])
        w_new = sb("w_new", [P, QT, H])
        w_wide = probs[:].rearrange("p a q h k -> p (a q h k)").rearrange("p (s a q h d) -> p s a q h d",
                                                                          s=2, a=2, q=QT, h=2)
        l_inv = sb("l_inv", [P, QT, H])
        oT = sb("oT", [P, B + 1, M, N])
        o_flat = oT[:].rearrange("p s m n -> p (s m n)")
        w2_sb = o_flat[:, B * M * N:].rearrange("p (e c d) -> p e c d", e=E, c=IC)
        b2_sb = o_flat[:, 0:E * D].rearrange("p (e d) -> p e d", e=E)
        b1_sb = v_sb[:].rearrange("p t n -> p (t n)").rearrange("p (e i) -> p e i", e=E)
        xn2 = wq_sb[:].rearrange("p c n -> p (c n)").rearrange("p (t d) -> p t d", d=D)
        routing = probs[:].rearrange("p a q h k -> p (a q h k)")
        routed = [0]

        def over_probs(shape, dt=F32):
            size = math.prod(shape[1:])
            part = routing[0:shape[0], routed[0]:routed[0] + size]
            routed[0] += size
            if dt != F32:
                part = part.bitcast(dt)
            if len(shape) == 2:
                return part
            return part.rearrange("p (a b) -> p a b", a=shape[1]) if len(shape) == 3 else part

        logits = over_probs([P, TT, E])
        lmax = over_probs([P, TT])
        first_w = sb("first_w", [P, E])
        ismax = over_probs([P, TT, E])
        onehot = over_probs([P, TT, E])
        earlier = over_probs([P, TT, E])
        count = over_probs([P, E])
        fills = over_probs([P, E, TT])
        tiles = over_probs([P, E])
        tile_sum = over_probs([P, E, E])
        tile_off = over_probs([P, E])
        place0 = over_probs([P, E])
        place_e = over_probs([P, TT, E])
        place_f = over_probs([P, TT])
        place = over_probs([P, TT], I32)
        tile_cmp = over_probs([1, NT + 2, E - 1])
        expert_f = over_probs([1, NT + 2])
        tiles_used = over_probs([1, 1])
        expert_code = over_probs([1, NT // 2 + 1], I32)
        pair_used = over_probs([1, NT // 2])
        pairs_f = over_probs([1, 1])
        pairs = over_probs([1, 1], I32)
        srow = o_flat[:, E * D:E * D + NT * RW].rearrange("p (t r) -> p t r", r=RW)
        sxn = o_flat[:, E * D + NT * RW:E * D + NT * RW + 2 * D].rearrange("p (s d) -> p s d", d=D)
        ffn = pT[:].rearrange("p a h k n -> p (a h k n)").rearrange("p (b s n) -> p b s n", b=4, s=2)
        sxT, h_pre, h_sb, hT = (ffn[:, i] for i in range(4))

        s_bank = [stack.enter_context(nc.psum_tensor(f"s_bank{i}", [P, 2, 512], F32)) for i in range(2)]
        one_bank = [stack.enter_context(nc.psum_tensor(f"bank{i}", [P, 512], F32)) for i in range(4)]
        bank = [s_bank[0][:, 0], s_bank[0][:, 1], s_bank[1][:, 0], s_bank[1][:, 1]] + [b[:] for b in one_bank]

        s_x = [sem(f"s_x{b}") for b in range(B)]
        s_wq = sem("s_wq")
        s_mask = [sem(f"s_mask{b}") for b in range(B)]
        s_wkv = sem("s_wkv")
        s_small = sem("s_small")
        s_ctx = sem("s_ctx")
        ident_ready = sem("ident_ready")
        pool_step = sem("pool_step")
        route_const = sem("route_const")
        var_ready = sem("var_ready")
        std_ready = sem("std_ready")
        ln_ready = sem("ln_ready")
        dve_step = sem("dve_step")
        pro_ps = sem("pro_ps")
        pro_act = sem("pro_act")
        pro_dve = sem("pro_dve")
        visit_part = sem("visit_part")
        visit_ps = sem("visit_ps")
        visit_ready = sem("visit_ready")
        gate_ready = sem("gate_ready")
        xb_ready = sem("xb_ready")
        proj_ps = sem("proj_ps")
        proj_act = sem("proj_act")
        proj_dve = sem("proj_dve")
        mask_ready = sem("mask_ready")
        scores_ready = sem("scores_ready")
        cmax_done = sem("cmax_done")
        negm_ready = sem("negm_ready")
        probs_ready = sem("probs_ready")
        ptrans_ready = sem("ptrans_ready")
        pT_act = sem("pT_act")
        pT_dve = sem("pT_dve")
        r_col_ready = sem("r_col_ready")
        rinv_ready = sem("rinv_ready")
        rinv_ps = sem("rinv_ps")
        rinv_taken = sem("rinv_taken")
        o_ready = sem("o_ready")
        o_taken = sem("o_taken")
        merge_arg = sem("merge_arg")
        merge_exp = sem("merge_exp")
        merge_step = sem("merge_step")
        merge_w = sem("merge_w")
        merge_ps = sem("merge_ps")
        merged = sem("merged")
        attn_done = sem("attn_done")
        state_copied = sem("state_copied")
        s_wo = sem("s_wo")
        s_w1 = sem("s_w1")
        s_w2 = sem("s_w2")
        q_ps = sem("q_ps")
        q_hi_ready = sem("q_hi_ready")
        q_lo_ready = sem("q_lo_ready")
        zeroed = sem("zeroed")
        wo_ready = sem("wo_ready")
        x2_ready = sem("x2_ready")
        xn2_ready = sem("xn2_ready")
        xt2_ps = sem("xt2_ps")
        xt2_sb = sem("xt2_sb")
        logit_ps = sem("logit_ps")
        count_ready = sem("count_ready")
        rank_ps = sem("rank_ps")
        place_ready = sem("place_ready")
        table_ready = sem("table_ready")
        s_empty = sem("s_empty")
        s_sorted = sem("s_sorted")
        s_rows = sem("s_rows")
        s_b1 = sem("s_b1")
        s_b2 = sem("s_b2")
        b2_ready = sem("b2_ready")
        empty_ready = sem("empty_ready")
        sxn_ready = sem("sxn_ready")
        sxT_ps = sem("sxT_ps")
        sxT_ready = sem("sxT_ready")
        h_ps = sem("h_ps")
        h_pre_ready = sem("h_pre_ready")
        h_ready = sem("h_ready")
        hT_ps = sem("hT_ps")
        hT_ready = sem("hT_ready")
        y_ps = sem("y_ps")
        y_taken = sem("y_taken")
        b2_added = sem("b2_added")
        s_out = sem("s_out")

        def chunk_dst(u):
            if u == 0:
                return ctxT.rearrange("p c k -> p (c k)")
            v = u - 1 - M // 2
            half = INNER // 512
            return v_sb[:, v // half, (v % half) * 512:(v % half + 1) * 512]

        head_rows = [slice(r * DH, (r + 1) * DH) for r in range(2)]

        def k_parts(k, u, rows_of):
            for r in range(2):
                yield (k[head_rows[rows_of[r]], 2 * u - 2:2 * u, r, :],
                       bank[u % 4][head_rows[r], :].rearrange("p (m k) -> p m k", k=CK))

        block = stack.enter_context(nc.Block())

        @block.sync
        def _(sp):
            def load_x(b):
                sp.dma_start(x_sb[:, b * QT:(b + 1) * QT, :],
                             x[b].rearrange("(q p) d -> p q d", p=P)).then_inc(s_x[b], 16)

            def load_mask(b):
                sp.dma_start(mask_sb[:, b * QT:(b + 1) * QT, :],
                             mask[b].rearrange("(q p) k -> p q k", p=P)).then_inc(s_mask[b], 16)

            load_x(0)
            sp.dma_start(wq_sb[:], wq.rearrange("(c p) n -> p c n", p=P)).then_inc(s_wq, 16)
            load_mask(0)
            for b in range(1, B):
                load_x(b)
                load_mask(b)
            sp.dma_start(wk_sb, wk.rearrange("(c p) n -> p c n", p=P)).then_inc(s_wkv, 16)
            sp.dma_start(wv_sb, wv.rearrange("(c p) n -> p c n", p=P)).then_inc(s_wkv, 16)
            done = sp.alloc_register("sp_done")
            sp.reg_mov(done, 0)
            left = sp.alloc_register("sp_left")
            chunk = sp.alloc_register("sp_chunk")
            for b in range(B):
                sp.wait_ge(visit_ready, b + 1)
                sp.reg_mov(left, sp.value_load(visit[0:1, b * (NC + 2):b * (NC + 2) + 1], min_val=1, max_val=NC))
                sp.reg_mov(chunk, sp.value_load(visit[0:1, b * (NC + 2) + 1:b * (NC + 2) + 2], min_val=0,
                                                max_val=NC - 1))
                with sp.Fori(0, NC) as i:
                    with sp.If(sp.snap(left) > 0):
                        c = sp.snap(chunk, min_val=0, max_val=NC - 1)
                        n = sp.snap(done)
                        sp.wait_ge(proj_ps, n * UNITS + 1)
                        sp.dma_start(ctx_sb[:], ctx_in[b, bass.ds(c * CK, CK), :]
                                     .rearrange("(t p) d -> p t d", p=P)).then_inc(s_ctx, 16)
                        sp.reg_mov(chunk, sp.value_load(visit[0:1, bass.ds(i + (b * (NC + 2) + 2), 1)], min_val=0,
                                                        max_val=NC - 1))
                        sp.reg_add(done, done, 1)
                        sp.reg_add(left, left, -1)
                    with sp.Else():
                        sp.nop()
                if b == 0:
                    sp.dma_start(wo_sb[:], wo.rearrange("(m p) d -> p m d", p=P)).then_inc(s_wo, 16)
                    sp.wait_ge(empty_ready, 2)
                    sp.dma_start(sorted_rows.rearrange("(t p) r -> p t r", p=P),
                                 empty_row[:].unsqueeze(1).broadcast_to([P, NT, RW])).then_inc(s_empty, 16)
            sp.wait_ge(x2_ready, QT)
            sp.dma_start(b2_sb, b2.unsqueeze(0).broadcast_to([P, E, D])).then_inc(s_b2, 16)
            n = sp.snap(done)
            sp.wait_ge(proj_ps, n * UNITS + 1)
            sp.dma_start(w1_sb, w1.rearrange("e (c p) i -> p e c i", p=P)).then_inc(s_w1, 16)
            sp.wait_ge(attn_done, B)
            sp.dma_start(b1_sb, b1.unsqueeze(0).broadcast_to([P, E, I])).then_inc(s_b1, 16)
            sp.dma_start(w2_sb, w2.rearrange("e (c p) d -> p e c d", p=P)).then_inc(s_w2, 16)
            sp.wait_ge(s_sorted, 16 * TT)
            sp.dma_start(srow[:, 0:2, :], sorted_rows[0:2 * P, :].rearrange("(t p) r -> p t r", p=P))\
                .then_inc(s_rows, 16)
            with sp.Fori(1, NT // 2) as i:
                sp.wait_ge(s_rows, i * 16)
                sp.dma_start(srow[:, bass.ds(2 * i, 2), :],
                             sorted_rows[bass.ds(2 * i * P, 2 * P), :].rearrange("(t p) r -> p t r", p=P))\
                    .then_inc(s_rows, 16)
            sp.wait_ge(s_rows, 16 * (NT // 2))

        @block.gpsimd
        def _(pool):
            nc.gpsimd.memset(ident[:], 0.0).then_inc(pool_step, 1)
            nc.gpsimd.memset(ident_bf[:], 0.0).then_inc(pool_step, 1)
            nc.gpsimd.memset(eps[:], EPS).then_inc(ident_ready, 1)
            nc.gpsimd.memset(ones[:], 1.0).then_inc(ident_ready, 1)
            for e in range(E):
                nc.gpsimd.memset(first_w[:, e:e + 1], float(E - e)).then_inc(ident_ready, 1)
            pool.wait_ge(pool_step, 2)
            for m in (ident, ident_bf):
                nc.gpsimd.affine_select(out=m[:], in_=m[:], compare_op=ALU.not_equal, fill=1.0, base=0,
                                        pattern=[[-1, P]], channel_multiplier=1).then_inc(ident_ready, 1)
            nc.gpsimd.iota(rows[:, :, TOKEN:RW].rearrange("p t o -> p (t o)").bitcast(I32), pattern=[[P, TT]], base=0,
                           channel_multiplier=1)
            nc.gpsimd.iota(tile_start[:], pattern=[[P, TT]], base=0, channel_multiplier=0,
                           allow_small_or_imprecise_dtypes=True)
            nc.gpsimd.iota(tile_no[:], pattern=[[1, NT + 2]], base=0, channel_multiplier=0,
                           allow_small_or_imprecise_dtypes=True)
            nc.gpsimd.iota(e_before[:], pattern=[[-1, E], [1, E]], base=0, channel_multiplier=0,
                           allow_small_or_imprecise_dtypes=True)
            nc.gpsimd.memset(before[:], 1.0).then_inc(pool_step, 1)
            pool.wait_ge(pool_step, 3)
            nc.gpsimd.tensor_scalar(e_before[:], e_before[:], 0.0, None, ALU.is_lt)
            nc.gpsimd.affine_select(out=before[:], in_=before[:], compare_op=ALU.is_gt, fill=0.0, base=0,
                                    pattern=[[1, P]], channel_multiplier=-1).then_inc(route_const, 1)
            nc.gpsimd.memset(k_lo[:].bitcast(F32), 0.0).then_inc(zeroed, 1)
            nc.gpsimd.memset(empty_row[:, 0:TOKEN], 0.0).then_inc(empty_ready, 1)
            nc.gpsimd.memset(empty_row[:, TOKEN:RW].bitcast(I32), NOWHERE).then_inc(empty_ready, 1)
            pool.wait_ge(gate_ready, 1)
            pool.wait_ge(ln_ready, TT)
            nc.gpsimd.tensor_scalar(bo_sb[:], bo_sb[:], gate[:, 0:1], None, ALU.mult).then_inc(pool_step, 1)
            pool.wait_ge(pool_step, 4)
            nc.gpsimd.tensor_tensor(x_sb, x_sb, bo_sb[:].unsqueeze(1).broadcast_to([P, TT, D]),
                                    ALU.add).then_inc(xb_ready, 1)
            pool.wait_ge(s_b2, 16)
            nc.gpsimd.tensor_scalar(b2_sb, b2_sb, gate[:, 1:2], None, ALU.mult).then_inc(b2_ready, 1)
            pool.wait_ge(s_empty, 16)
            pool.wait_ge(place_ready, 1)
            for tt in range(TT):
                nc.gpsimd.indirect_dma_start(out=sorted_rows, in_=rows[:, tt, :], in_offset=None,
                                             out_offset=bass.IndirectOffsetOnAxis(ap=place[:, tt:tt + 1], axis=0))\
                    .then_inc(s_sorted, 16)
            out_rows = out.rearrange("b n d -> (b n) d")
            pool.wait_ge(table_ready, 1)
            written = pool.alloc_register("pool_written")
            pool.reg_mov(written, 0)
            used = pool.value_load(pairs[0:1, 0:1], min_val=TT // 2, max_val=NT // 2)
            for i in range(NT // 2):
                with pool.If(used > i):
                    for s in range(2 * i, 2 * i + 2):
                        pool.wait_ge(y_taken, s + 3)
                        nc.gpsimd.indirect_dma_start(out=out_rows, in_=srow[:, s, 0:D], in_offset=None,
                                                     out_offset=bass.IndirectOffsetOnAxis(
                                                         ap=srow[:, s, TOKEN:RW].bitcast(I32), axis=0),
                                                     bounds_check=T - 1, oob_is_err=False).then_inc(s_out, 16)
                    pool.reg_add(written, written, 32)
                with pool.Else():
                    pool.nop()
            pool.wait_ge(s_out, pool.snap(written))

        @block.scalar
        def _(act):
            act.dma_start(gate_in[:, 0:1], g_xattn.unsqueeze(0).broadcast_to([P, 1])).then_inc(s_small, 16)
            act.dma_start(gate_in[:, 1:2], g_ffn.unsqueeze(0).broadcast_to([P, 1])).then_inc(s_small, 16)
            act.dma_start(bo_sb[:], bo.unsqueeze(0).broadcast_to([P, D])).then_inc(s_small, 16)
            act.dma_start(bg_sb[:], bg.unsqueeze(0).broadcast_to([P, E])).then_inc(s_small, 16)
            act.dma_start(wg_sb[:], wg.rearrange("(c p) e -> p c e", p=P)).then_inc(s_small, 16)
            act.wait_ge(ident_ready, E + 4)
            nc.scalar.activation(warm[:], eps[:], ACT.Sqrt)

            def std1(b):
                act.wait_ge(var_ready, b + 1)
                nc.scalar.activation(std[:, b * QT:(b + 1) * QT],
                                     rows[:, b * QT:(b + 1) * QT, VAR:VAR + 1].rearrange("p t o -> p (t o)"), ACT.Sqrt,
                                     bias=eps[:]).then_inc(std_ready, 1)

            def std2(tt):
                act.wait_ge(var_ready, B + tt + 1)
                nc.scalar.activation(std[:, tt:tt + 1], rows[:, tt, VAR:VAR + 1], ACT.Sqrt,
                                     bias=eps[:]).then_inc(std_ready, 1)

            def take_xt2(tt):
                act.wait_ge(xt2_ps, tt + 1)
                nc.scalar.copy(xnT[:, :, tt * P:(tt + 1) * P],
                               bank[2 + tt % 2][:, 0:D].rearrange("p (c n) -> p c n", c=DC)).then_inc(xt2_sb, 1)

            std1(0)
            act.wait_ge(pro_ps, 1)
            nc.scalar.copy(xnT[:, 0, 0:N], bank[4]).then_inc(pro_act, 1)
            done = act.alloc_register("act_done")
            act.reg_mov(done, 0)
            left = act.alloc_register("act_left")
            merges = act.alloc_register("act_merges")
            act.reg_mov(merges, 0)
            later = act.alloc_register("act_later")
            for b in range(B):
                for m in range(M):
                    act.wait_ge(q_ps, b * M + m + 1)
                    for h in range(2):
                        nc.scalar.copy(q_parts[head_rows[h], m, h, :], bank[m % 4][head_rows[h], :])\
                            .then_inc(q_hi_ready, 1)
                    if b == 0 and m == 1:
                        std1(1)
                        act.wait_ge(s_small, 16 * 5)
                        nc.scalar.activation(gate[:], gate_in[:], ACT.Tanh).then_inc(gate_ready, 1)
                act.reg_mov(later, 0)
                if b == 0:
                    act.wait_ge(pro_ps, 3)
                    nc.scalar.copy(xnT[:, 0, N:T], bank[4]).then_inc(pro_act, 1)
                    act.wait_ge(pro_ps, 4)
                    nc.scalar.copy(xnT[:, 1, N:T], bank[5]).then_inc(pro_act, 1)
                else:
                    for q in range(QT):
                        std2(q)
                act.wait_ge(visit_ready, b + 1)
                act.reg_mov(left, act.value_load(visit[0:1, b * (NC + 2):b * (NC + 2) + 1], min_val=1, max_val=NC))
                with act.Fori(0, NC) as i:
                    with act.If(act.snap(left) > 0):
                        n = act.snap(done)
                        units = n * UNITS
                        g = n * PER
                        act.wait_ge(proj_ps, units + 2)
                        nc.scalar.copy(chunk_dst(0), bank[0]).then_inc(proj_act, 1)
                        for u in range(1, 1 + M // 2):
                            act.wait_ge(proj_ps, units + (u + 2))
                            for rows_of in ((0, 1), (1, 0)):
                                for dst, src in k_parts(k_hi, u, rows_of):
                                    last = nc.scalar.copy(dst, src)
                            last.then_inc(proj_act, 1)

                        def take_v(u):
                            act.wait_ge(proj_ps, units + (u + 2))
                            nc.scalar.copy(chunk_dst(u), bank[u - 1]).then_inc(proj_act, 1)

                        take_v(1 + M // 2)

                        def take_pT(u):
                            act.wait_ge(ptrans_ready, g * 2 + (2 * u + 1))
                            act.wait_ge(o_ready, g + (max(u - 1, 0) + 1))
                            nc.scalar.copy(pT[:, u % 2, 0].rearrange("p t n -> p (t n)"), bank[4]).then_inc(pT_act, 1)

                        def take_rinv(u):
                            act.wait_ge(rinv_ps, g + (u + 1))
                            act.wait_ge(o_taken, g + (max(u - 1, 0) + 1))
                            nc.scalar.copy(rinv_b[:, u % 2, :], bank[7][:, 0:CK]).then_inc(rinv_taken, 1)

                        for u in range(PER):
                            m, j = u // 2, u % 2
                            act.wait_ge(negm_ready, g + (u + 1))
                            for i in range(2):
                                if i == 1 and u >= 1:
                                    take_pT(u - 1)
                                if i == 0 and u >= 2:
                                    act.wait_ge(ptrans_ready, g * 2 + 2 * (u - 1))
                                for h in range(2):
                                    col = negm[:, 2 * j + i, 2 * m + h:2 * m + h + 1]
                                    last = nc.scalar.activation(probs[:, u % 2, i, h, :],
                                                                s_bank[u % 2][:, i, h * CK:(h + 1) * CK], ACT.Exp,
                                                                bias=col, scale=SCALE,
                                                                accum_out=lsum[:, 2 * j + i, 2 * m + h:2 * m + h + 1])
                            last.then_inc(probs_ready, 1)
                            if u == 0:
                                take_v(3 + M // 2)
                            if u >= 1:
                                take_rinv(u - 1)
                        take_pT(PER - 1)
                        take_rinv(PER - 1)
                        act.reg_add(done, done, 1)
                        act.reg_add(left, left, -1)
                        with act.If(act.snap(later) > 0):
                            k = act.snap(merges)
                            act.wait_ge(merge_arg, k + 1)
                            nc.scalar.activation(w_old[:], w_old[:], ACT.Exp)
                            nc.scalar.activation(w_new[:], w_new[:], ACT.Exp).then_inc(merge_exp, 1)
                            act.reg_add(merges, merges, 1)
                        with act.Else():
                            act.nop()
                        act.reg_mov(later, 1)
                    with act.Else():
                        act.nop()
            for q in range(QT):
                take_xt2(q)
            for q in range(QT):
                std2(QT + q)
                if q >= 1:
                    take_xt2(QT + q - 1)
            take_xt2(TT - 1)
            act.wait_ge(table_ready, 1)
            act.reg_mov(left, act.value_load(pairs[0:1, 0:1], min_val=TT // 2, max_val=NT // 2))
            with act.Fori(0, NT // 2) as i:
                with act.If(act.snap(left) > 0):
                    for s in range(2):
                        act.wait_ge(h_pre_ready, 2 * i + (s + 1))
                        nc.scalar.activation(h_sb[:, s, :], h_pre[:, s, :], ACT.Gelu).then_inc(h_ready, 1)
                    for s in range(2):
                        act.wait_ge(hT_ps, 2 * i + (s + 1))
                        act.wait_ge(y_ps, 2 * i + (s + 1))
                        nc.scalar.copy(hT[:, s, :], bank[4 + s][:, 0:I]).then_inc(hT_ready, 1)
                    act.reg_add(left, left, -1)
                with act.Else():
                    act.nop()

        @block.vector
        def _(dve):
            steps, stds = [0], [0]
            dve.sem_inc(o_taken, 1)
            dve.sem_inc(y_taken, 2)

            def then(ins):
                steps[0] += 1
                ins.then_inc(dve_step, 1)
                dve.wait_ge(dve_step, steps[0])

            def variance(tiles):
                for t in tiles:
                    last = nc.vector.bn_stats(stats[:, t, :], x_sb[:, t, :])
                then(last)
                for t in tiles:
                    last = nc.vector.bn_aggr(rows[:, t, MEAN:MEAN + 2], stats[:, t, :])
                last.then_inc(var_ready, 1)

            def norm(a, z, dst, ready):
                stds[0] += 1
                dve.wait_ge(std_ready, stds[0])
                then(nc.vector.reciprocal(rows[:, a:z, RSTD:RSTD + 1].rearrange("p t o -> p (t o)"), std[:, a:z]))
                for t in range(a, z):
                    nc.vector.tensor_scalar(dst[:, t, :], x_sb[:, t, :], rows[:, t, MEAN:MEAN + 1],
                                            rows[:, t, RSTD:RSTD + 1], ALU.subtract, ALU.mult).then_inc(ready, 1)

            def take_q(b, m):
                dve.wait_ge(q_hi_ready, (b * M + m + 1) * 2)
                for h in range(2):
                    nc.vector.tensor_tensor(q_parts[head_rows[1 - h], m, h, :], bank[m % 4][head_rows[h], :],
                                            q_parts[head_rows[h], m, h, :].bitcast(F32), ALU.subtract)\
                        .then_inc(q_lo_ready, 1)

            def any_visible(b):
                tiles_b = slice(b * QT, (b + 1) * QT)
                dve.wait_ge(s_mask[b], 16)
                for t in range(b * QT, (b + 1) * QT, 2):
                    pairs = mask_sb[:, t:t + 2, :].rearrange("p t k -> p (t k)").bitcast(U16)
                    last = nc.vector.tensor_reduce(rowmin[:, t:t + 2, :].rearrange("p t c -> p (t c)"),
                                                   pairs.rearrange("p (n k) -> p n k", k=CK // 2), AX.X, ALU.min)
                then(last)
                then(nc.vector.tensor_scalar(rowmin[:, tiles_b], rowmin[:, tiles_b], 257.0, None, ALU.is_ge))
                nc.vector.tensor_reduce(chunkmin[:, b], rowmin[:, tiles_b].rearrange("p q c -> p c q"), AX.X, ALU.min)
                then(nc.vector.tensor_reduce(fullrow[:, tiles_b], rowmin[:, tiles_b], AX.X, ALU.min))
                then(nc.vector.tensor_reduce(fullb[:, b:b + 1], fullrow[:, tiles_b], AX.X, ALU.max))
                nc.vector.tensor_tensor(visit_p[:, b], fullb[:, b:b + 1].broadcast_to([P, NC]), chunkmin[:, b],
                                        ALU.subtract).then_inc(visit_part, 1)

            def to_visit(b):
                dve.wait_ge(route_const, 1)
                dve.wait_ge(visit_ps, b + 1)
                then(nc.vector.tensor_scalar(visited[:], bank[6 - b][0:1, 0:NC], -P + 0.5, None, ALU.is_gt))
                then(nc.vector.tensor_tensor(visit_cmp[:, 0:NC, :], visited[:].unsqueeze(1).broadcast_to([1, NC, NC]),
                                             e_before[0:1, 1:NC + 1, 0:NC], ALU.mult))
                then(nc.vector.tensor_reduce(visit_cum[:], visit_cmp[:, 0:NC, :], AX.X, ALU.add))
                then(nc.vector.tensor_tensor(visit_cmp[:, :, 0:NC - 1],
                                             visit_cum[:, 0:NC - 1].unsqueeze(1).broadcast_to([1, NC + 1, NC - 1]),
                                             tile_no[:, 0:NC + 1].unsqueeze(2).broadcast_to([1, NC + 1, NC - 1]),
                                             ALU.is_le))
                then(nc.vector.tensor_reduce(visit_no[:], visit_cmp[:, :, 0:NC - 1], AX.X, ALU.add))
                at = b * (NC + 2)
                nc.vector.tensor_copy(visit[:, at:at + 1], visit_cum[:, NC - 1:NC])
                nc.vector.tensor_copy(visit[:, at + 1:at + NC + 2], visit_no[:]).then_inc(visit_ready, 1)

            dve.wait_ge(s_x[0], 16)
            variance(range(QT))
            norm(0, QT, xn, ln_ready)
            dve.wait_ge(pro_ps, 2)
            nc.vector.tensor_copy(xnT[:, 1, 0:N], bank[5]).then_inc(pro_dve, 1)
            any_visible(0)
            take_q(0, 0)
            take_q(0, 1)
            dve.wait_ge(s_x[1], 16)
            variance(range(QT, TT))
            to_visit(0)
            take_q(0, 2)
            take_q(0, 3)
            norm(QT, TT, xn, ln_ready)
            for m in range(4, M):
                take_q(0, m)
            done = dve.alloc_register("dve_done")
            dve.reg_mov(done, 0)
            left = dve.alloc_register("dve_left")
            chunk = dve.alloc_register("dve_chunk")
            merges = dve.alloc_register("dve_merges")
            dve.reg_mov(merges, 0)
            later = dve.alloc_register("dve_later")

            def route(b):
                half = slice(b * QT, (b + 1) * QT)
                shape = [P, QT, E]
                dve.wait_ge(logit_ps, b + 1)
                then(nc.vector.tensor_tensor(logits[:, half], bank[4 + b][:, 0:QT * E]
                                             .rearrange("p (t e) -> p t e", e=E),
                                             bg_sb[:].unsqueeze(1).broadcast_to(shape), ALU.add))
                then(nc.vector.tensor_reduce(lmax[:, half], logits[:, half], AX.X, ALU.max))
                then(nc.vector.tensor_tensor(ismax[:, half], logits[:, half],
                                             lmax[:, half].unsqueeze(2).broadcast_to(shape), ALU.is_equal))
                then(nc.vector.tensor_tensor(ismax[:, half], ismax[:, half],
                                             first_w[:].unsqueeze(1).broadcast_to(shape), ALU.mult))
                then(nc.vector.tensor_reduce(lmax[:, half], ismax[:, half], AX.X, ALU.max))
                then(nc.vector.tensor_tensor(onehot[:, half], ismax[:, half],
                                             lmax[:, half].unsqueeze(2).broadcast_to(shape), ALU.is_equal))
                if b == 0:
                    then(nc.vector.memset(earlier[:, 0, :], 0.0))
                    for tt in range(1, QT + 1):
                        then(nc.vector.tensor_tensor(earlier[:, tt, :], earlier[:, tt - 1, :], onehot[:, tt - 1, :],
                                                     ALU.add))
                else:
                    nc.vector.tensor_reduce(count, onehot.rearrange("p t e -> p e t"), AX.X, ALU.add)\
                        .then_inc(count_ready, 1)

            def after_attention(b):
                for tt in range(b * QT, (b + 1) * QT):
                    dve.wait_ge(wo_ready, tt + 1)
                    nc.vector.scalar_tensor_tensor(x_sb[:, tt, :], bank[6 + tt % 2][:, 0:D], gate[:, 0:1], x_sb[:, tt, :],
                                                   ALU.mult, ALU.add).then_inc(x2_ready, 1)
                    dve.wait_ge(x2_ready, tt + 1)
                    variance([tt])
                    norm(tt, tt + 1, xn2, xn2_ready)
                    if tt == QT + 1:
                        route(0)

            for b in range(B):
                if b == 0:
                    dve.wait_ge(zeroed, 1)
                else:
                    for m in range(M):
                        take_q(b, m)
                        if m == 1:
                            any_visible(b)
                    to_visit(b)
                    dve.wait_ge(xb_ready, 1)
                    after_attention(b - 1)
                dve.reg_mov(later, 0)
                dve.wait_ge(visit_ready, b + 1)
                dve.reg_mov(left, dve.value_load(visit[0:1, b * (NC + 2):b * (NC + 2) + 1], min_val=1, max_val=NC))
                dve.reg_mov(chunk, dve.value_load(visit[0:1, b * (NC + 2) + 1:b * (NC + 2) + 2], min_val=0,
                                                max_val=NC - 1))
                with dve.Fori(0, NC) as i:
                    with dve.If(dve.snap(left) > 0):
                        c = dve.snap(chunk, min_val=0, max_val=NC - 1)
                        n = dve.snap(done)
                        slot = dve.snap(dve.snap(later, min_val=0, max_val=1) * (B - b) + b, min_val=0, max_val=B)
                        units = n * UNITS
                        g = n * PER
                        dve.wait_ge(scores_ready, g + 1)
                        nc.vector.tensor_scalar(maskneg[:], mask_sb[:, b * QT:(b + 1) * QT, bass.ds(c * CK, CK)],
                                                -BIG, None, ALU.mult).then_inc(mask_ready, 1)
                        dve.reg_mov(chunk, dve.value_load(visit[0:1, bass.ds(i + (b * (NC + 2) + 2), 1)], min_val=0,
                                                        max_val=NC - 1))
                        for u in range(1, 1 + M // 2):
                            dve.wait_ge(proj_act, n * UNITS_ACT + (u + 1))
                            for (dst, src), (hi, _) in zip(k_parts(k_lo, u, (0, 1)), k_parts(k_hi, u, (0, 1))):
                                last = nc.vector.tensor_tensor(dst, src, hi.bitcast(F32), ALU.subtract)
                            last.then_inc(proj_dve, 1)

                        def take_v(u):
                            dve.wait_ge(proj_ps, units + (u + 2))
                            nc.vector.tensor_copy(chunk_dst(u), bank[u - 1]).then_inc(proj_dve, 1)

                        def take_max(u):
                            m, j = u // 2, u % 2
                            dve.wait_ge(scores_ready, g + (u + 2))
                            nc.vector.tensor_reduce(cmax[:, u % 2], s_bank[u % 2][:].rearrange("p i (h k) -> p i h k", h=2),
                                                    AX.X, ALU.max).then_inc(cmax_done, 1)
                            dve.wait_ge(cmax_done, g + (u + 1))
                            nc.vector.tensor_scalar(negm[:, 2 * j:2 * j + 2, 2 * m:2 * m + 2], cmax[:, u % 2], -SCALE,
                                                    None, ALU.mult).then_inc(negm_ready, 1)

                        def take_sum(u):
                            m, j = u // 2, u % 2
                            dve.wait_ge(probs_ready, g + (u + 1))
                            nc.vector.reciprocal(r_col[:, u % 2], lsum[:, 2 * j:2 * j + 2, 2 * m:2 * m + 2])\
                                .then_inc(r_col_ready, 1)
                            dve.wait_ge(r_col_ready, g + (u + 1))
                            nc.vector.tensor_copy(rinv[:, u % 2], r_col[:, u % 2].unsqueeze(3)
                                                  .broadcast_to([P, 2, 2, DH]))\
                                .then_inc(rinv_ready, 1)

                        def take_pT(u):
                            dve.wait_ge(ptrans_ready, g * 2 + (2 * u + 2))
                            dve.wait_ge(o_ready, g + (max(u - 1, 0) + 1))
                            nc.vector.tensor_copy(pT[:, u % 2, 1].rearrange("p t n -> p (t n)"), bank[5]).then_inc(pT_dve, 1)

                        def take_o(u):
                            m, j = u // 2, u % 2
                            dve.wait_ge(o_ready, g + (u + 2))
                            dve.wait_ge(rinv_taken, g + (u + 1))
                            dst = oT[:].rearrange("p s m n -> p s (m n)")[:, bass.ds(slot, 1),
                                                                          m * N + j * CK:m * N + (j + 1) * CK]
                            nc.vector.tensor_tensor(dst.rearrange("p s n -> p (s n)"), bank[6][:, 0:CK], rinv_b[:, u % 2, :],
                                                    ALU.mult).then_inc(o_taken, 1)

                        take_v(2 + M // 2)
                        take_max(0)
                        take_v(4 + M // 2)
                        for u in range(PER):
                            if u + 1 < PER:
                                take_max(u + 1)
                            take_sum(u)
                            take_pT(u)
                            if u >= 1:
                                take_o(u - 1)
                        take_o(PER - 1)
                        dve.reg_add(done, done, 1)
                        dve.reg_add(left, left, -1)
                        with dve.If(dve.snap(later) > 0):
                            k = dve.snap(merges)
                            ks = k * 6
                            nc.vector.tensor_tensor(negm_new[:], negm_run[:], negm[:], ALU.min).then_inc(merge_step, 1)
                            dve.wait_ge(merge_step, ks + 1)
                            nc.vector.tensor_tensor(w_old[:], negm_new[:], negm_run[:], ALU.subtract)
                            nc.vector.tensor_tensor(w_new[:], negm_new[:], negm[:], ALU.subtract).then_inc(merge_arg, 1)
                            dve.wait_ge(merge_exp, k + 1)
                            nc.vector.tensor_copy(negm_run[:], negm_new[:])
                            nc.vector.tensor_tensor(w_old[:], w_old[:], l_run[:], ALU.mult)
                            nc.vector.tensor_tensor(w_new[:], w_new[:], lsum[:], ALU.mult).then_inc(merge_step, 1)
                            dve.wait_ge(merge_step, ks + 2)
                            nc.vector.tensor_tensor(l_run[:], w_old[:], w_new[:], ALU.add).then_inc(merge_step, 1)
                            dve.wait_ge(merge_step, ks + 3)
                            nc.vector.reciprocal(l_inv[:], l_run[:]).then_inc(merge_step, 1)
                            dve.wait_ge(merge_step, ks + 4)
                            nc.vector.tensor_tensor(w_old[:], w_old[:], l_inv[:], ALU.mult)
                            nc.vector.tensor_tensor(w_new[:], w_new[:], l_inv[:], ALU.mult).then_inc(merge_step, 1)
                            dve.wait_ge(merge_step, ks + 5)

                            def widen(m):
                                for a, w in enumerate((w_old, w_new)):
                                    last = nc.vector.tensor_copy(w_wide[:, m % 2, a], w[:, :, 2 * m:2 * m + 2]
                                                                 .unsqueeze(3).broadcast_to([P, QT, 2, DH]))
                                last.then_inc(merge_w, 1)

                            widen(0)
                            for m in range(M):
                                if m + 1 < M:
                                    if m >= 1:
                                        dve.wait_ge(merge_ps, k * M + m)
                                    widen(m + 1)
                                dve.wait_ge(merge_ps, k * M + (m + 1))
                                nc.vector.tensor_tensor(oT[:, b, m, :], oT[:, b, m, :], s_bank[m % 2][:, 0], ALU.mult)
                                nc.vector.tensor_tensor(oT[:, B, m, :], oT[:, B, m, :], s_bank[m % 2][:, 1], ALU.mult)\
                                    .then_inc(merged, 1)
                                dve.wait_ge(merged, k * M + (m + 1))
                                last = nc.vector.tensor_tensor(oT[:, b, m, :], oT[:, b, m, :], oT[:, B, m, :], ALU.add)
                            last.then_inc(merge_step, 1)
                            dve.wait_ge(merge_step, ks + 6)
                            dve.reg_add(merges, merges, 1)
                        with dve.Else():
                            nc.vector.tensor_copy(negm_run[:], negm[:])
                            nc.vector.tensor_copy(l_run[:], lsum[:]).then_inc(state_copied, 1)
                            dve.wait_ge(state_copied, b + 1)
                        dve.reg_mov(later, 1)
                    with dve.Else():
                        dve.nop()
                nc.vector.memset(cmax[:], 0.0).then_inc(attn_done, 1)
            after_attention(B - 1)
            route(1)
            for tt in range(QT + 1, TT):
                then(nc.vector.tensor_tensor(earlier[:, tt, :], earlier[:, tt - 1, :], onehot[:, tt - 1, :], ALU.add))
            dve.wait_ge(rank_ps, 1)
            then(nc.vector.tensor_tensor(fills, bank[4][:, E:2 * E].unsqueeze(2).broadcast_to([P, E, TT]),
                                         tile_start[:].unsqueeze(1).broadcast_to([P, E, TT]), ALU.is_gt))
            then(nc.vector.tensor_reduce(tiles, fills, AX.X, ALU.add))
            then(nc.vector.tensor_tensor(tile_sum, tiles.unsqueeze(1).broadcast_to([P, E, E]), e_before[:],
                                         ALU.mult))
            then(nc.vector.tensor_reduce(tile_off, tile_sum, AX.X, ALU.add))
            then(nc.vector.scalar_tensor_tensor(place0, tile_off, float(P), bank[4][:, 0:E], ALU.mult, ALU.add))
            then(nc.vector.tensor_tensor(place_e, earlier, place0.unsqueeze(1).broadcast_to([P, TT, E]),
                                         ALU.add))
            then(nc.vector.tensor_tensor(place_e, place_e, onehot, ALU.mult))
            then(nc.vector.tensor_reduce(place_f, place_e, AX.X, ALU.add))
            nc.vector.tensor_copy(place, place_f).then_inc(place_ready, 1)
            then(nc.vector.tensor_tensor(tile_cmp, tile_off[0:1, 1:E].unsqueeze(1).broadcast_to([1, NT + 2, E - 1]),
                                         tile_no[:].unsqueeze(2).broadcast_to([1, NT + 2, E - 1]), ALU.is_le))
            nc.vector.tensor_reduce(expert_f, tile_cmp, AX.X, ALU.add)
            then(nc.vector.tensor_tensor(tiles_used, tile_off[0:1, E - 1:E], tiles[0:1, E - 1:E], ALU.add))
            pair_expert = expert_f.rearrange("p (i s) -> p i s", s=2)
            nc.vector.scalar_tensor_tensor(expert_code, pair_expert[:, :, 1], float(E), pair_expert[:, :, 0], ALU.mult,
                                           ALU.add)
            then(nc.vector.tensor_tensor(pair_used, tile_no[:, 0:NT].rearrange("p (i s) -> p i s", s=2)[:, :, 0],
                                         tiles_used.broadcast_to([1, NT // 2]), ALU.is_lt))
            then(nc.vector.tensor_reduce(pairs_f, pair_used, AX.X, ALU.add))
            nc.vector.tensor_copy(pairs, pairs_f).then_inc(table_ready, 1)
            dve.wait_ge(table_ready, 1)

            def norm_pair(i):
                dve.wait_ge(s_rows, i * 16 + 16)
                for s in range(2):
                    row = srow[:, bass.ds(2 * i + s, 1), :].rearrange("p t r -> p (t r)")
                    nc.vector.tensor_scalar(sxn[:, s, :], row[:, 0:D], row[:, MEAN:MEAN + 1], row[:, RSTD:RSTD + 1],
                                            ALU.subtract, ALU.mult).then_inc(sxn_ready, 1)

            def take_sxT(i):
                for s in range(2):
                    dve.wait_ge(sxT_ps, 2 * i + (s + 1))
                    nc.vector.tensor_copy(sxT[:, s, :], bank[s][:, 0:D]).then_inc(sxT_ready, 1)

            next_experts = [dve.alloc_register(f"dve_expert{s}") for s in range(2)]

            def load_experts(i):
                code = dve.value_load(expert_code[0:1, bass.ds(i, 1)], min_val=0, max_val=E * E - 1)
                dve.reg_mov(next_experts[0], code % E)
                dve.reg_mov(next_experts[1], code // E)

            def expert_pair(i, more):
                with dve.If(dve.snap(left) > 0):
                    experts = [dve.snap(r, min_val=0, max_val=E - 1) for r in next_experts]
                    for s, e in enumerate(experts):
                        dve.wait_ge(h_ps, 2 * i + (s + 1))
                        nc.vector.tensor_tensor(h_pre[:, s, :], bank[2 + s][:, 0:I],
                                                b1_sb[:, bass.ds(e, 1), :].rearrange("p e i -> p (e i)"),
                                                ALU.add).then_inc(h_pre_ready, 1)
                    if more:
                        norm_pair(i + 1)
                    out_rows = [srow[:, bass.ds(2 * i + s, 1), :].rearrange("p t r -> p (t r)")[:, 0:D] for s in range(2)]
                    for row, e in zip(out_rows, experts):
                        nc.vector.tensor_tensor(row, row, b2_sb[:, bass.ds(e, 1), :].rearrange("p e d -> p (e d)"),
                                                ALU.add).then_inc(b2_added, 1)
                    if more:
                        take_sxT(i + 1)
                        load_experts(i + 1)
                    for s, row in enumerate(out_rows):
                        dve.wait_ge(b2_added, 2 * i + (s + 1))
                        dve.wait_ge(y_ps, 2 * i + (s + 3))
                        nc.vector.scalar_tensor_tensor(row, bank[6 + s][:, 0:D], gate[:, 1:2], row, ALU.mult,
                                                       ALU.add).then_inc(y_taken, 1)
                    dve.reg_add(left, left, -1)
                with dve.Else():
                    dve.nop()

            dve.reg_mov(left, dve.value_load(pairs[0:1, 0:1], min_val=TT // 2, max_val=NT // 2))
            load_experts(0)
            dve.wait_ge(s_b1, 16)
            dve.wait_ge(b2_ready, 1)
            norm_pair(0)
            take_sxT(0)
            with dve.Fori(0, NT // 2 - 1) as i:
                expert_pair(i, True)
            expert_pair(NT // 2 - 1, False)

        @block.tensor
        def _(pe):
            pe.sem_inc(proj_ps, 1)
            pe.sem_inc(scores_ready, 1)
            pe.sem_inc(o_ready, 1)
            pe.sem_inc(y_ps, 2)
            pe.wait_ge(ident_ready, E + 4)

            def xn_transposes(b):
                for i in range(QT):
                    pe.wait_ge(ln_ready, b * QT + i + 1)
                    for c in range(DC):
                        last = nc.tensor.transpose(bank[4 + c][:, i * P:(i + 1) * P],
                                                   xn[:, b * QT + i, c * P:(c + 1) * P], ident[:])
                        if i == QT - 1:
                            last.then_inc(pro_ps, 1)

            def visit_sum(b):
                pe.wait_ge(visit_part, b + 1)
                nc.tensor.matmul(bank[6 - b][0:1, 0:NC], ones[:, 0:1], visit_p[:, b, :], start=True, stop=True)\
                    .then_inc(visit_ps, 1)

            xn_transposes(0)
            pe.wait_ge(s_wq, 16)
            pe.wait_ge(pro_act, 1)
            done = pe.alloc_register("pe_done")
            pe.reg_mov(done, 0)
            left = pe.alloc_register("pe_left")
            merges = pe.alloc_register("pe_merges")
            pe.reg_mov(merges, 0)
            later = pe.alloc_register("pe_later")

            def project_tile(tt):
                b, q = tt // QT, tt % QT
                if q >= 2:
                    pe.wait_ge(x2_ready, tt - 1)
                for m in range(M):
                    last = nc.tensor.matmul(bank[6 + tt % 2][:, 0:D], oT[:, b, m, q * P:(q + 1) * P], wo_sb[:, m, :],
                                            start=(m == 0), stop=(m == M - 1))
                last.then_inc(wo_ready, 1)

            def output_projection(b):
                pe.wait_ge(s_wo, 16)
                pe.wait_ge(attn_done, b + 1)
                for q in range(QT):
                    project_tile(b * QT + q)
                pe.wait_ge(x2_ready, (b + 1) * QT)

            def xn2_transposes(tt):
                pe.wait_ge(xn2_ready, tt + 1)
                if tt >= 2:
                    pe.wait_ge(xt2_sb, tt - 1)
                for c in range(DC):
                    last = nc.tensor.transpose(bank[2 + tt % 2][:, c * P:(c + 1) * P], xn2[:, tt, c * P:(c + 1) * P],
                                               ident[:])
                last.then_inc(xt2_ps, 1)

            def tile_logits(tt):
                pe.wait_ge(xt2_sb, tt + 1)
                for c in range(DC):
                    last = nc.tensor.matmul(bank[4 + tt // QT][:, (tt % QT) * E:(tt % QT + 1) * E], xnT[:, c, tt * P:(tt + 1) * P],
                                            wg_sb[:, c, :], start=(c == 0), stop=(c == DC - 1))
                return last

            for b in range(B):
                for m in range(M):
                    if m >= 4:
                        pe.wait_ge(q_lo_ready, (b * M + m - 3) * 2)
                    for c in range(DC):
                        if b == 0 and m == 0 and c == 1:
                            pe.wait_ge(pro_dve, 1)
                        last = nc.tensor.matmul(bank[m % 4], wq_sb[:, c, m * P:(m + 1) * P],
                                                xnT[:, c, b * N:(b + 1) * N], start=(c == 0), stop=(c == DC - 1))
                    last.then_inc(q_ps, 1)
                    if m == 2 + 4 * b:
                        visit_sum(b)
                if b == 0:
                    xn_transposes(1)
                    pe.wait_ge(s_wkv, 32)
                else:
                    output_projection(b - 1)
                pe.wait_ge(visit_ready, b + 1)
                pe.wait_ge(q_lo_ready, (b * M + M - 3) * 2)
                pe.reg_mov(later, 0)
                pe.reg_mov(left, pe.value_load(visit[0:1, b * (NC + 2):b * (NC + 2) + 1], min_val=1, max_val=NC))
                with pe.Fori(0, NC) as i:
                    with pe.If(pe.snap(left) > 0):
                        n = pe.snap(done)
                        g = n * PER
                        ua, ud = n * UNITS_ACT, n * UNITS_DVE
                        pe.wait_ge(s_ctx, n * 16 + 16)
                        for c in range(DC):
                            for t in range(KT):
                                last = nc.tensor.transpose(bank[0][:, c * CK + t * P:c * CK + (t + 1) * P],
                                                           ctx_sb[:, t, c * P:(c + 1) * P], ident[:])
                        last.then_inc(proj_ps, 1)
                        pe.wait_ge(proj_act, ua + 1)
                        pe.wait_ge(q_lo_ready, (b + 1) * M * 2)
                        pe.wait_ge(pro_act, 3)
                        for u in range(1, 1 + M // 2):
                            for i in range(2):
                                m = 2 * (u - 1) + i
                                for c in range(DC):
                                    last = nc.tensor.matmul(bank[u % 4][:, i * CK:(i + 1) * CK],
                                                            wk_sb[:, c, m * P:(m + 1) * P], ctxT[:, c, :],
                                                            start=(c == 0), stop=(c == DC - 1))
                            last.then_inc(proj_ps, 1)

                        def project_v(units):
                            pe.wait_ge(o_taken, g + 1)
                            for u in units:
                                v = u - 1 - M // 2
                                t, half = v // (INNER // 512), v % (INNER // 512)
                                for c in range(DC):
                                    last = nc.tensor.matmul(bank[4 + v], ctxT[:, c, t * P:(t + 1) * P],
                                                            wv_sb[:, c, half * 512:(half + 1) * 512],
                                                            start=(c == 0), stop=(c == DC - 1))
                                last.then_inc(proj_ps, 1)

                        def scores(u):
                            if u >= 2:
                                pe.wait_ge(probs_ready, g + (u - 1))
                            m, j = u // 2, u % 2
                            for i in range(2):
                                q = 2 * j + i
                                s = s_bank[u % 2][:, i, :]
                                nc.tensor.matmul(s.rearrange("p (h k) -> p h k", h=2), ident_bf[:],
                                                 maskneg[:, q, :].unsqueeze(1).broadcast_to([P, 2, CK]),
                                                 start=True, stop=False)
                                for h in range(2):
                                    for k in (k_lo, k_hi):
                                        last = nc.tensor.matmul(s[:, h * CK:(h + 1) * CK],
                                                                q_parts[:, m, h, q * P:(q + 1) * P], k[:, m, h, :],
                                                                start=False, stop=(h == 1 and k is k_hi))
                            last.then_inc(scores_ready, 1)

                        def transposes(u):
                            pe.wait_ge(probs_ready, g + (u + 1))
                            if u >= 1:
                                pe.wait_ge(pT_act, g + u)
                                pe.wait_ge(pT_dve, g + u)
                            for h in range(2):
                                for t in range(KT):
                                    for i in range(2):
                                        last = nc.tensor.transpose(bank[4 + h][:, t * CK + i * P:t * CK + (i + 1) * P],
                                                                   probs[:, u % 2, i, h, t * P:(t + 1) * P], ident[:])
                                last.then_inc(ptrans_ready, 1)

                        def values(u):
                            m = u // 2
                            pe.wait_ge(rinv_ready, g + (u + 1))
                            if u >= 1:
                                pe.wait_ge(rinv_taken, g + u)
                            else:
                                pe.wait_ge(o_taken, g + 1)
                            for i in range(2):
                                last = nc.tensor.transpose(bank[7][:, i * P:(i + 1) * P],
                                                           rinv[:, u % 2, i].rearrange("p h d -> p (h d)"), ident[:])
                            last.then_inc(rinv_ps, 1)
                            pe.wait_ge(pT_act, g + (u + 1))
                            pe.wait_ge(pT_dve, g + (u + 1))
                            pe.wait_ge(o_taken, g + (u + 1))
                            for t in range(KT):
                                for h in range(2):
                                    last = nc.tensor.matmul(bank[6][h * DH:(h + 1) * DH, 0:CK],
                                                            v_sb[:, t, (2 * m + h) * DH:(2 * m + h + 1) * DH],
                                                            pT[:, u % 2, h, t, :], start=(t == 0), stop=(t == KT - 1))
                            last.then_inc(o_ready, 1)

                        project_v(range(1 + M // 2, 3 + M // 2))
                        pe.wait_ge(proj_dve, ud + M // 2)
                        pe.wait_ge(mask_ready, n + 1)
                        scores(0)
                        project_v(range(3 + M // 2, UNITS))
                        scores(1)
                        pe.wait_ge(proj_act, ua + UNITS_ACT)
                        pe.wait_ge(proj_dve, ud + UNITS_DVE)
                        for u in range(PER):
                            if 2 <= u + 1 < PER:
                                scores(u + 1)
                            if u >= 1:
                                values(u - 1)
                            transposes(u)
                        values(PER - 1)
                        pe.reg_add(done, done, 1)
                        pe.reg_add(left, left, -1)
                        with pe.If(pe.snap(later) > 0):
                            k = pe.snap(merges)
                            for m in range(M):
                                pe.wait_ge(merge_w, k * M + (m + 1))
                                if m >= 2:
                                    pe.wait_ge(merged, k * M + (m - 1))
                                for a in range(2):
                                    for q in range(QT):
                                        last = nc.tensor.transpose(s_bank[m % 2][:, a, q * P:(q + 1) * P],
                                                                   w_wide[:, m % 2, a, q]
                                                                   .rearrange("p h d -> p (h d)"), ident[:])
                                last.then_inc(merge_ps, 1)
                            pe.wait_ge(merged, k * M + M)
                            pe.reg_add(merges, merges, 1)
                        with pe.Else():
                            pe.nop()
                        pe.reg_mov(later, 1)
                    with pe.Else():
                        pe.nop()
            for tt in range(QT):
                xn2_transposes(tt)
            pe.wait_ge(attn_done, B)
            project_tile(QT)
            for tt in range(QT):
                last = tile_logits(tt)
            last.then_inc(logit_ps, 1)
            project_tile(QT + 1)
            xn2_transposes(QT)
            for q in range(2, QT):
                project_tile(QT + q)
                tile_logits(QT + q - 2)
                xn2_transposes(QT + q - 1)
            tile_logits(TT - 2)
            xn2_transposes(TT - 1)
            tile_logits(TT - 1).then_inc(logit_ps, 1)
            pe.wait_ge(route_const, 1)
            pe.wait_ge(count_ready, 1)
            nc.tensor.matmul(bank[4][:, 0:E], before[:], count, start=True, stop=True)
            nc.tensor.matmul(bank[4][:, E:2 * E], ones[:], count, start=True, stop=True).then_inc(rank_ps, 1)
            pe.wait_ge(s_w1, 16)
            pe.wait_ge(s_w2, 16)
            pe.wait_ge(table_ready, 1)
            pe.reg_mov(left, pe.value_load(pairs[0:1, 0:1], min_val=TT // 2, max_val=NT // 2))
            next_experts = [pe.alloc_register(f"pe_expert{s}") for s in range(2)]

            def load_experts(i):
                code = pe.value_load(expert_code[0:1, bass.ds(i, 1)], min_val=0, max_val=E * E - 1)
                pe.reg_mov(next_experts[0], code % E)
                pe.reg_mov(next_experts[1], code // E)

            def pair_transposes(i):
                for s in range(2):
                    pe.wait_ge(sxn_ready, 2 * i + (s + 1))
                    for c in range(DC):
                        last = nc.tensor.transpose(bank[s][:, c * P:(c + 1) * P], sxn[:, s, c * P:(c + 1) * P], ident[:])
                    last.then_inc(sxT_ps, 1)

            def expert_pair(i, more):
                with pe.If(pe.snap(left) > 0):
                    e = [pe.snap(r, min_val=0, max_val=E - 1) for r in next_experts]
                    for s in range(2):
                        pe.wait_ge(sxT_ready, 2 * i + (s + 1))
                        for c in range(DC):
                            last = nc.tensor.matmul(bank[2 + s][:, 0:I], sxT[:, s, c * P:(c + 1) * P],
                                                    w1_sb[:, bass.ds(e[s], 1), c, :].rearrange("p e i -> p (e i)"),
                                                    start=(c == 0), stop=(c == DC - 1))
                        last.then_inc(h_ps, 1)
                    if more:
                        load_experts(i + 1)
                    for s in range(2):
                        pe.wait_ge(h_ready, 2 * i + (s + 1))
                        for ic in range(IC):
                            last = nc.tensor.transpose(bank[4 + s][:, ic * P:(ic + 1) * P],
                                                       h_sb[:, s, ic * P:(ic + 1) * P], ident[:])
                        last.then_inc(hT_ps, 1)
                    if more:
                        pair_transposes(i + 1)
                    for s in range(2):
                        pe.wait_ge(hT_ready, 2 * i + (s + 1))
                        pe.wait_ge(y_taken, 2 * i + (s + 1))
                        for ic in range(IC):
                            last = nc.tensor.matmul(bank[6 + s][:, 0:D], hT[:, s, ic * P:(ic + 1) * P],
                                                    w2_sb[:, bass.ds(e[s], 1), ic, :].rearrange("p e d -> p (e d)"),
                                                    start=(ic == 0), stop=(ic == IC - 1))
                        last.then_inc(y_ps, 1)
                    pe.reg_add(left, left, -1)
                with pe.Else():
                    pe.nop()

            load_experts(0)
            pair_transposes(0)
            with pe.Fori(0, NT // 2 - 1) as i:
                expert_pair(i, True)
            expert_pair(NT // 2 - 1, False)


_INS = ['x', 'ctx_1024', 'mask_BxSxS2_bk1', 'g_xattn', 'g_ffn', 'L0_xattn_Wq', 'L0_xattn_Wk', 'L0_xattn_Wv',
        'L0_xattn_Wo', 'L0_xattn_bo', 'L0_ffn_Wg', 'L0_ffn_bg', 'L0_ffn_W1', 'L0_ffn_b1', 'L0_ffn_W2', 'L0_ffn_b2']


def kernel(**inputs):
    import numpy as _np
    import concourse.bacc as _bacc
    from concourse import mybir as _mybir
    from concourse.bass_utils import run_bass_kernel_spmd as _run

    nc = _bacc.Bacc("TRN2", target_bir_lowering=False, num_devices=1)
    arrays, args = {}, []
    for name in _INS:
        a = _np.ascontiguousarray(inputs[name])
        arrays[f"in_{name}_dram"] = a
        args.append(nc.dram_tensor(f"in_{name}_dram", a.shape, _mybir.dt.from_np(a.dtype), kind="ExternalInput").ap())
    shape = inputs['x'].shape
    args.append(nc.dram_tensor("out_0_dram", shape, _mybir.dt.float32, kind="ExternalOutput").ap())
    flamingo_kernel(nc, *args)
    r = _run(nc, [arrays], core_ids=[0])
    return r.results[0]["out_0_dram"]
```
